# Optimizing a Trainium2 kernel written in Bass

```python
import numpy as np
import jax
import jax.numpy as jnp

def _softmax(x, axis=-1):
    return jax.nn.softmax(x, axis=axis)

def _gelu(x):
    return jax.nn.gelu(x, approximate=True)

def _silu(x):
    return jax.nn.silu(x)

def _sigmoid(x):
    return jax.nn.sigmoid(x)

def _layernorm(x, axis=-1, eps=1e-05):
    m = jnp.mean(x, axis=axis, keepdims=True)
    v = jnp.var(x, axis=axis, keepdims=True)
    return (x - m) / jnp.sqrt(v + eps)

def _scatter_add(tgt, idx, src, axis=0):
    return tgt.at[idx].add(src)

def _segment_sum(src, seg, n):
    return jax.ops.segment_sum(src, seg, n)
kernel_name = 'mk_decoder_postln_d1_seqx_r8_ee6d6b'

def setup_inputs(seed: int=0):
    np.random.seed(seed)
    _w = jnp.asarray

    def _rec_inputs():
        import jax
        import jax.numpy as jnp
        _rk = jax.random.key(seed)
        x = -0.0002928 + 1 * jax.random.normal(jax.random.fold_in(_rk, 1), (2, 512, 128), jnp.float32)
        _lenS = 512 - jax.random.randint(jax.random.fold_in(_rk, 7), (2,), 0, max(1, 512 // 4) + 1, jnp.int32)
        _lenS2 = 154 - jax.random.randint(jax.random.fold_in(_rk, 8), (2,), 0, max(1, 154 // 4) + 1, jnp.int32)
        _ctx_1024P = jax.random.normal(jax.random.fold_in(_rk, 11), (2, 16, 128), jnp.float32)
        _ctx_1024c = jax.random.dirichlet(jax.random.fold_in(_rk, 511), 0.3 * jnp.ones((16,), jnp.float32), (2, 154))
        _ctx_1024t = jnp.einsum('bsk,bkd->bsd', _ctx_1024c, _ctx_1024P)
        _ctx_1024t = _ctx_1024t * jax.lax.rsqrt(jnp.mean(jnp.square(_ctx_1024t)) + 1e-12) * 0.953939
        ctx_1024 = -1.39393e-06 + 0.999914 * (_ctx_1024t + 0.3 * jax.random.normal(jax.random.fold_in(_rk, 611), (2, 154, 128), jnp.float32))
        return (x, ctx_1024)
    x, ctx_1024 = _rec_inputs()

    def _L0_attn_setup():
        import jax, jax.numpy as jnp
        import numpy as np
        import math
        B, N, D = (2, 256, 128)
        H = 16
        DH = D // H
        CG_ITERS = 30
        THRESHOLD = 0.99
        LAMBDA_INIT = 1.0
        LAMBDA_LOWER = 0.25
        NORM_EPS = 1e-05

        def l2norm(x, eps=1e-06):
            return x * jax.lax.rsqrt(jnp.sum(x * x, axis=-1, keepdims=True) + eps)

        def cg_solve(A, rhs, n_iters):
            x0 = jnp.zeros_like(rhs)
            rs0 = jnp.sum(rhs * rhs, axis=-1)

            def step(carry, _):
                x, r, p, rs = carry
                Ap = jnp.einsum('bhij,bhj->bhi', A, p)
                alpha = rs / (jnp.sum(p * Ap, axis=-1) + 1e-12)
                x = x + alpha[..., None] * p
                r = r - alpha[..., None] * Ap
                rs_new = jnp.sum(r * r, axis=-1)
                p = r + (rs_new / (rs + 1e-12))[..., None] * p
                return ((x, r, p, rs_new), None)
            (x, _, _, _), _ = jax.lax.scan(step, (x0, rhs, rhs, rs0), None, length=n_iters)
            return x
        key = jax.random.key(seed)
        ks = jax.random.split(key, 10)
        std = 0.02
        inp = {'x': jax.random.normal(ks[0], (B, N, D), dtype=jnp.float32), 'Wq': jax.random.normal(ks[1], (D, D), dtype=jnp.float32) * std, 'Wk': jax.random.normal(ks[2], (D, D), dtype=jnp.float32) * std, 'Wv': jax.random.normal(ks[3], (D, D), dtype=jnp.float32) * std, 'Wf': jax.random.normal(ks[4], (D, H), dtype=jnp.float32) * std, 'Wbet': jax.random.normal(ks[5], (D, H), dtype=jnp.float32) * std, 'Wo': jax.random.normal(ks[6], (D, D), dtype=jnp.float32) * std, 'delta': jnp.full((H,), math.log(THRESHOLD / (1.0 - THRESHOLD)), dtype=jnp.float32), 'lamb_params': jnp.full((D,), math.log(math.exp(math.exp(LAMBDA_INIT - LAMBDA_LOWER)) - 1.0), dtype=jnp.float32), 'norm_weight': jnp.ones((D,), dtype=jnp.float32), 'gate_w1': jax.random.normal(ks[7], (D, DH), dtype=jnp.float32) * std, 'gate_w2': jax.random.normal(ks[8], (DH, D), dtype=jnp.float32) * std}
        return inp
    _L0_attn_all = _L0_attn_setup()
    _L0_attn_in = {k: v for k, v in _L0_attn_all.items() if k in ('Wq', 'Wk', 'Wv', 'Wf', 'Wbet', 'Wo', 'delta', 'lamb_params', 'norm_weight', 'gate_w1', 'gate_w2')}
    del _L0_attn_all

    def _L0_xattn_setup():
        import jax, jax.numpy as jnp
        import numpy as np
        D_MODEL = 128
        NUM_HEADS = 16
        D_K = D_MODEL // NUM_HEADS

        def _split_heads(x):
            B, S, D = x.shape
            return x.reshape(B, S, NUM_HEADS, D_K).transpose(0, 2, 1, 3)
        key = jax.random.key(seed)
        ks = jax.random.split(key, 11)
        B, S, D = (2, 256, D_MODEL)
        s = 1.0 / np.sqrt(D)
        return {'Q': jax.random.normal(ks[0], (B, S, D), jnp.float32), 'K': jax.random.normal(ks[1], (B, S, D), jnp.float32), 'V': jax.random.normal(ks[2], (B, S, D), jnp.float32), 'Wq': jax.random.normal(ks[3], (D, D), jnp.float32) * s, 'bq': jax.random.normal(ks[4], (D,), jnp.float32) * s, 'Wk': jax.random.normal(ks[5], (D, D), jnp.float32) * s, 'bk': jax.random.normal(ks[6], (D,), jnp.float32) * s, 'Wv': jax.random.normal(ks[7], (D, D), jnp.float32) * s, 'bv': jax.random.normal(ks[8], (D,), jnp.float32) * s, 'Wo': jax.random.normal(ks[9], (D, D), jnp.float32) * s, 'bo': jax.random.normal(ks[10], (D,), jnp.float32) * s}
    _L0_xattn_all = _L0_xattn_setup()
    _L0_xattn_in = {k: v for k, v in _L0_xattn_all.items() if k in ('Wq', 'bq', 'Wk', 'bk', 'Wv', 'bv', 'Wo', 'bo')}
    del _L0_xattn_all

    def _L0_ffn_setup():
        import jax, jax.numpy as jnp
        import numpy as np
        B, L, D = (4, 64, 128)
        E, TOP_K = (16, 4)
        F = 4 * D
        key = jax.random.key(seed)
        ks = jax.random.split(key, 6)
        scale = 0.02
        return {'x': jax.random.normal(ks[0], (B, L, D), jnp.float32), 'keys': jax.random.normal(ks[1], (E, D), jnp.float32), 'w1': jax.random.normal(ks[2], (E, F, D), jnp.float32) * scale, 'b1': jnp.zeros((E, F), jnp.float32), 'w2': jax.random.normal(ks[3], (E, D, F), jnp.float32) * scale, 'b2': jnp.zeros((E, D), jnp.float32), 'rw': jax.random.normal(ks[4], (E, D), jnp.float32) * scale, 'rb': jnp.zeros((E,), jnp.float32)}
    _L0_ffn_all = _L0_ffn_setup()
    _L0_ffn_in = {k: v for k, v in _L0_ffn_all.items() if k in ('keys', 'w1', 'b1', 'w2', 'b2', 'rw', 'rb')}
    del _L0_ffn_all
    return {'x': x, 'ctx_1024': ctx_1024, 'L0_attn_Wq': _L0_attn_in['Wq'], 'L0_attn_Wk': _L0_attn_in['Wk'], 'L0_attn_Wv': _L0_attn_in['Wv'], 'L0_attn_Wf': _L0_attn_in['Wf'], 'L0_attn_Wbet': _L0_attn_in['Wbet'], 'L0_attn_Wo': _L0_attn_in['Wo'], 'L0_attn_delta': _L0_attn_in['delta'], 'L0_attn_lamb_params': _L0_attn_in['lamb_params'], 'L0_attn_norm_weight': _L0_attn_in['norm_weight'], 'L0_attn_gate_w1': _L0_attn_in['gate_w1'], 'L0_attn_gate_w2': _L0_attn_in['gate_w2'], 'L0_xattn_Wq': _L0_xattn_in['Wq'], 'L0_xattn_bq': _L0_xattn_in['bq'], 'L0_xattn_Wk': _L0_xattn_in['Wk'], 'L0_xattn_bk': _L0_xattn_in['bk'], 'L0_xattn_Wv': _L0_xattn_in['Wv'], 'L0_xattn_bv': _L0_xattn_in['bv'], 'L0_xattn_Wo': _L0_xattn_in['Wo'], 'L0_xattn_bo': _L0_xattn_in['bo'], 'L0_ffn_keys': _L0_ffn_in['keys'], 'L0_ffn_w1': _L0_ffn_in['w1'], 'L0_ffn_b1': _L0_ffn_in['b1'], 'L0_ffn_w2': _L0_ffn_in['w2'], 'L0_ffn_b2': _L0_ffn_in['b2'], 'L0_ffn_rw': _L0_ffn_in['rw'], 'L0_ffn_rb': _L0_ffn_in['rb']}

def reference(x, ctx_1024, L0_attn_Wq, L0_attn_Wk, L0_attn_Wv, L0_attn_Wf, L0_attn_Wbet, L0_attn_Wo, L0_attn_delta, L0_attn_lamb_params, L0_attn_norm_weight, L0_attn_gate_w1, L0_attn_gate_w2, L0_xattn_Wq, L0_xattn_bq, L0_xattn_Wk, L0_xattn_bk, L0_xattn_Wv, L0_xattn_bv, L0_xattn_Wo, L0_xattn_bo, L0_ffn_keys, L0_ffn_w1, L0_ffn_b1, L0_ffn_w2, L0_ffn_b2, L0_ffn_rw, L0_ffn_rb):
    import jax
    import jax.numpy as jnp

    def _L0_attn_ref(x, Wq, Wk, Wv, Wf, Wbet, Wo, delta, lamb_params, norm_weight, gate_w1, gate_w2):
        import jax, jax.numpy as jnp
        import numpy as np
        import math
        B, N, D = (2, 256, 128)
        H = 16
        DH = D // H
        CG_ITERS = 30
        THRESHOLD = 0.99
        LAMBDA_INIT = 1.0
        LAMBDA_LOWER = 0.25
        NORM_EPS = 1e-05

        def l2norm(x, eps=1e-06):
            return x * jax.lax.rsqrt(jnp.sum(x * x, axis=-1, keepdims=True) + eps)

        def cg_solve(A, rhs, n_iters):
            x0 = jnp.zeros_like(rhs)
            rs0 = jnp.sum(rhs * rhs, axis=-1)

            def step(carry, _):
                x, r, p, rs = carry
                Ap = jnp.einsum('bhij,bhj->bhi', A, p)
                alpha = rs / (jnp.sum(p * Ap, axis=-1) + 1e-12)
                x = x + alpha[..., None] * p
                r = r - alpha[..., None] * Ap
                rs_new = jnp.sum(r * r, axis=-1)
                p = r + (rs_new / (rs + 1e-12))[..., None] * p
                return ((x, r, p, rs_new), None)
            (x, _, _, _), _ = jax.lax.scan(step, (x0, rhs, rhs, rs0), None, length=n_iters)
            return x
        b, n, d = x.shape
        h, dh = (H, DH)
        q = (x @ Wq).reshape(b, n, h, dh)
        k = (x @ Wk).reshape(b, n, h, dh)
        v = (x @ Wv).reshape(b, n, h, dh)
        log_f = jax.nn.log_sigmoid(x @ Wf + delta)
        beta = jax.nn.sigmoid(x @ Wbet)
        lamb = (jax.nn.softplus(lamb_params) + LAMBDA_LOWER).reshape(h, dh)
        q = l2norm(q)
        k = l2norm(k)
        diag_lamb = lamb[:, :, None] * jnp.eye(dh, dtype=x.dtype)
        qT = q.transpose(1, 0, 2, 3)
        kT = k.transpose(1, 0, 2, 3)
        vT = v.transpose(1, 0, 2, 3)
        fT = log_f.transpose(1, 0, 2)
        bT = beta.transpose(1, 0, 2)

        def step(carry, inp):
            h_kk, h_kv = carry
            qt, kt, vt, ft, bt = inp
            fexp = jnp.exp(ft)[..., None, None]
            bkt = bt[..., None] * kt
            h_kk = fexp * h_kk + jnp.einsum('bhi,bhj->bhij', bkt, kt)
            h_kv = fexp * h_kv + jnp.einsum('bhi,bhj->bhij', bkt, vt)
            A = h_kk + diag_lamb
            qs = cg_solve(A, qt, CG_ITERS)
            ot = jnp.einsum('bhi,bhij->bhj', qs, h_kv)
            return ((h_kk, h_kv), ot)
        init = (jnp.zeros((b, h, dh, dh), dtype=x.dtype), jnp.zeros((b, h, dh, dh), dtype=x.dtype))
        _, oT = jax.lax.scan(step, init, (qT, kT, vT, fT, bT))
        o = oT.transpose(1, 0, 2, 3)
        gate = jax.nn.sigmoid(x @ gate_w1 @ gate_w2).reshape(b, n, h, dh)
        og = o * gate
        og = og * jax.lax.rsqrt(jnp.mean(og * og, axis=-1, keepdims=True) + NORM_EPS)
        out = og.reshape(b, n, d) * norm_weight
        return out @ Wo

    def _L0_xattn_ref(Q, K, V, Wq, bq, Wk, bk, Wv, bv, Wo, bo):
        import jax, jax.numpy as jnp
        import numpy as np
        D_MODEL = 128
        NUM_HEADS = 16
        D_K = D_MODEL // NUM_HEADS

        def _split_heads(x):
            B, S, D = x.shape
            return x.reshape(B, S, NUM_HEADS, D_K).transpose(0, 2, 1, 3)
        q = _split_heads(Q @ Wq + bq)
        k = _split_heads(K @ Wk + bk)
        v = _split_heads(V @ Wv + bv)
        scale = 1.0 / np.sqrt(D_K)
        scores = jnp.einsum('bhqd,bhkd->bhqk', q, k) * scale
        P = jax.nn.softmax(scores, axis=-1)
        O = jnp.einsum('bhqk,bhkd->bhqd', P, v)
        B, H, S, dk = O.shape
        O = O.transpose(0, 2, 1, 3).reshape(B, S, H * dk)
        return O @ Wo + bo

    def _L0_ffn_ref(x, keys, w1, b1, w2, b2, rw, rb):
        import jax, jax.numpy as jnp
        import numpy as np
        B, L, D = (4, 64, 128)
        E, TOP_K = (16, 4)
        F = 4 * D
        diff = x[:, :, None, :] - keys
        dist2 = jnp.sum(diff * diff, axis=-1)
        logits = -dist2 + jnp.einsum('bld,ed->ble', x, rw) + rb
        topv, topi = jax.lax.top_k(logits, TOP_K)
        w = jax.nn.softmax(topv, axis=-1)
        hidden = jax.nn.gelu(jnp.einsum('bld,efd->blef', x, w1) + b1, approximate=False)
        exp_out = jnp.einsum('blef,edf->bled', hidden, w2) + b2
        sel = jnp.take_along_axis(exp_out, topi[..., None], axis=2)
        fused = jnp.sum(w[..., None] * sel, axis=2)
        return fused
    x = _layernorm(x + _L0_attn_ref(x, L0_attn_Wq, L0_attn_Wk, L0_attn_Wv, L0_attn_Wf, L0_attn_Wbet, L0_attn_Wo, L0_attn_delta, L0_attn_lamb_params, L0_attn_norm_weight, L0_attn_gate_w1, L0_attn_gate_w2), axis=-1)
    x = _layernorm(x + _L0_xattn_ref(x, ctx_1024, ctx_1024, L0_xattn_Wq, L0_xattn_bq, L0_xattn_Wk, L0_xattn_bk, L0_xattn_Wv, L0_xattn_bv, L0_xattn_Wo, L0_xattn_bo), axis=-1)
    x = _layernorm(x + _L0_ffn_ref(x, L0_ffn_keys, L0_ffn_w1, L0_ffn_b1, L0_ffn_w2, L0_ffn_b2, L0_ffn_rw, L0_ffn_rb), axis=-1)
    return x

_drawn_inputs = setup_inputs


def setup_inputs(seed=0):
    import zlib

    import numpy as np

    out = dict(_drawn_inputs(seed))
    spreads = {'L0_attn_delta': (4.595119953155518, 0.2),
     'L0_attn_lamb_params': (1.9887207746505737, 0.6),
     'L0_attn_norm_weight': (1.0, 0.2),
     'L0_ffn_b1': (0.0, 0.336),
     'L0_ffn_b2': (0.0, 0.1),
     'L0_ffn_rb': (0.0, 0.8)}
    factors = {'L0_attn_Wf': 8.0,
     'L0_attn_Wbet': 3.148,
     'L0_attn_gate_w1': 8.0,
     'L0_attn_gate_w2': 8.0,
     'L0_xattn_bq': 2.717,
     'L0_xattn_bk': 8.0,
     'L0_ffn_rw': 8.0}
    for name, (base, spread) in spreads.items():
        noise = np.random.default_rng([zlib.crc32(name.encode()), seed]).standard_normal(out[name].shape)
        drawn = base * np.exp(spread * noise) if base else spread * noise
        out[name] = jnp.asarray(drawn.astype(out[name].dtype))
    for name, factor in factors.items():
        out[name] = (out[name] * factor).astype(out[name].dtype)
    return out
```

```python
from contextlib import ExitStack

import concourse.bass as bass
from concourse import mybir

F32 = mybir.dt.float32
U32 = mybir.dt.uint32
ALU = mybir.AluOpType
ACT = mybir.ActivationFunctionType
AX = mybir.AxisListType

P = 128
B, S, D = 2, 512, 128
H, DH = 16, 8
TB = S // P
G = TB * H
C = 154
CR = C - P
NQ = H // 4
E, F = 16, 512
FC = F // P
TOPK = 4
LAMBDA_LOWER = 0.25
L2_EPS = 1e-6
NORM_EPS = 1e-5
SM_SCALE = DH ** -0.5
LNEXP = "natural_log_exp_and_others"


def bc(ap, axis, n):
    v = ap.unsqueeze(axis)
    shape = list(v.shape)
    shape[axis] = n
    return v.broadcast_to(tuple(shape))


def decoder_layer(nc, xTok, xT, ctxT, wqkv, wsmall, gw2, wo, cols, rowsb, xw, keysrw, b2, w1T, w2T, b1T, consts, out):
    ctx = ExitStack()
    with ctx:
        def sb(name, shape, dt=F32):
            return ctx.enter_context(nc.sbuf_tensor(name, shape, dt))

        def sem(name):
            return ctx.enter_context(nc.semaphore(name))

        PS = ctx.enter_context(nc.psum_tensor("PS", [P, 8, 512], F32))

        epst = sb("epst", [P, 2])
        x_sb = sb("x_sb", [P, B, TB, D])
        xT_sb = sb("xT_sb", [P, B, S])
        ctxT_sb = sb("ctxT_sb", [P, B, C])
        wqkv_sb = sb("wqkv_sb", [P, 3, D])
        wsmall_sb = sb("wsmall_sb", [P, 2 * H + DH])
        gw2_sb = sb("gw2_sb", [DH, D])
        wo_sb = sb("wo_sb", [P, D])
        cols_sb = sb("cols_sb", [P, 6])
        rows_sb = sb("rows_sb", [P, 3 * D + E])
        xw_sb = sb("xw_sb", [P, 4, D])
        keysrw_sb = sb("keysrw_sb", [P, 2, E])
        b2_sb = sb("b2_sb", [E, D])
        const_sb = sb("const_sb", [P, 2 * P + DH * P + DH + E])
        delta_col, normw_col = cols_sb[:, 0:1], cols_sb[:, 1:2]
        lamb_row, bv_row, bo_row = (rows_sb[:, i * D:(i + 1) * D] for i in range(3))
        rb_row = rows_sb[:, 3 * D:3 * D + E]
        ident = const_sb[:, 0:P]
        headones = const_sb[:, P:2 * P]
        sel = const_sb[:, 2 * P:2 * P + DH * P].rearrange("p (j n) -> p j n", j=DH)
        hmask = const_sb[:, 2 * P + DH * P:2 * P + DH * P + DH]
        iota = const_sb[:, 2 * P + DH * P + DH:2 * P + DH * P + DH + E]
        wq = wqkv_sb[:, 0, :]
        gw1 = wsmall_sb[:, 2 * H:2 * H + DH]
        xwq, xwk, xwv, xwo = (xw_sb[:, i, :] for i in range(4))

        wrep = sb("wrep", [P, 2, DH, D])
        wfb = sb("wfb", [P, 2, D])
        lamb = sb("lamb", [P, D])
        softtmp = sb("softtmp", [P, D])
        onesq = sb("onesq", [P, P])
        rcomb = sb("rcomb", [P, E])
        keysq = sb("keysq", [P, E])
        cE = sb("cE", [P, E])
        kx = sb("kx", [64, 2, B * C])
        Kb = sb("Kb", [72, B, 2, DH, C])
        Kr = sb("Kr", [72, B, 2, DH, 32])
        ctxR = sb("ctxR", [P, B, 4, 32])
        Vm = sb("Vm", [P, B, H, 32])
        Vr = sb("Vr", [P, B, NQ, 4, 32])
        nmx = sb("nmx", [P, TB, 2, 72])

        fgt = sb("fgt", [P, S])
        beta = sb("beta", [P, S])
        gateh = sb("gateh", [DH, S])
        gateT = sb("gateT", [P, S])
        sq = sb("sq", [P, S])
        qsq = sb("qsq", [P, S])
        kinv = sb("kinv", [P, S])
        kbeta = sb("kbeta", [P, S])
        kc = sb("kc", [P, S])
        prod = sb("prod", [P, S])
        qss = sb("qss", [P, G])
        qinv = sb("qinv", [P, G])
        Akk = sb("Akk", [P, DH, S])
        Akv = sb("Akv", [P, DH, S])
        M = sb("M", [P, DH, DH + 1, G])
        U = sb("U", [P, DH, DH + 1, G])
        tmp = sb("tmp", [P, DH - 1, DH, G])
        rpiv = sb("rpiv", [P, G])
        og = qsq
        attn = prod

        res = sb("res", [P, TB, D])
        stats = sb("stats", [P, TB, 6])
        mv = sb("mv", [P, TB, 2])
        rstd = sb("rstd", [P, TB])
        x1 = sb("x1", [P, TB, D])
        x1b = sb("x1b", [P, TB, D])
        xsol = kc
        x1T = kc
        Qx = sb("Qx", [72, 2, S])
        Pm = Akk[:].rearrange("p j s -> p (j s)")[:, 0:6 * S].rearrange("p (r k s) -> p r k s", r=3, k=2)
        tmpf = tmp[:].rearrange("p i j g -> p (i j g)")
        Osb = tmpf[:, 0:NQ * S].rearrange("p (q s) -> p q s", q=NQ)
        Pr = tmpf[:, NQ * S:(NQ + 2) * S].rearrange("p (k s) -> p k s", k=2)
        rden = sb("rden", [P, TB * H])
        On = sb("On", [P, TB * H, DH])
        OnT = kbeta

        x2 = sb("x2", [P, B, TB, D])
        x2T = sb("x2T", [P, B, S])
        xsq = sb("xsq", [P, TB])
        logit = sb("logit", [P, TB, E])
        top8 = sb("top8", [P, TB, 8])
        idx8 = sb("idx8", [P, TB, 8], U32)
        idx4 = sb("idx4", [P, TB, TOPK])
        w4 = sb("w4", [P, TB, TOPK])
        wsum = sb("wsum", [P, TB])
        oneh = sb("oneh", [P, TB * TOPK, E])
        gates = sb("gates", [P, B * TB, E])
        gatesT = sb("gatesT", [E, S])
        gslot = sb("gslot", [P, 2, B * TB])
        w1_sb = sb("w1_sb", [P, 2, F])
        w2_sb = sb("w2_sb", [P, 2, FC, D])
        b1_sb = sb("b1_sb", [P, 2, FC])
        hid = U[:, :, :, :].rearrange("p i j g -> p (i j g)")[:, 0:2 * FC * S].rearrange(
            "p (r c s) -> p r c s", r=2, c=FC)
        acc = x2
        fin = x_sb

        names = """ld_attn ld_late setup_ready wrep_ready lamb_exp lamb_ln proj_ready f_ready beta_ready gh_ready
        gate_ready ksq_ready qsq_ready ksum_ready kinv_ready kvec_ready qss_ready qinv_ready rep_ready rep_used
        kk_ready tr_ready m_ready qn_ready solved qsT_ready okv_ready oT_ready og_ready ogsq_ready ogms_ready
        ogr_ready attn_ready attny_ready stats_ready rstd_ready x1_ready x1T_ready x1T_sb xq_ready xq_sb ms_ready
        mx_ready nm_ready nm_sb sc_ready p_ready pv_done ox_sb xt_ready on_ready onT_ready onT_sb xy_ready x2_ready
        x2T_ready x2T_sb lg_ready xsq_ready w4_diff w4_ready g_ready gT_ready gT_sb acc_in_ready acc_init
        kx_ready kx_sb kb_ready ctxR_ready vx_ready v_ready key_ready keysq_ready
        dve_chain act_chain h_ready gelu_ready y_ready acc_done out_done fin_ready
        pool_set gslot_ready"""
        s = {n: sem(n) for n in names.split()}
        ld_w = [sem(f"ld_w{i}") for i in range(2)]

        block = ctx.enter_context(nc.Block())
        N_ATTN, N_LATE = 10, 6

        @block.sync
        def _(sp):
            for dst, src in ((xT_sb, xT), (wqkv_sb, wqkv), (wsmall_sb, wsmall), (cols_sb, cols), (gw2_sb, gw2),
                             (const_sb, consts), (rows_sb[:, 0:D], rowsb[0]), (x_sb, xTok), (wo_sb, wo),
                             (ctxT_sb, ctxT)):
                sp.dma_start(dst[:], src).then_inc(s["ld_attn"], 16)
            for dst, src in ((rows_sb[:, D:2 * D], rowsb[1]), (rows_sb[:, 2 * D:3 * D], rowsb[2]),
                             (rows_sb[:, 3 * D:], rowsb[3]), (xw_sb, xw), (keysrw_sb, keysrw), (b2_sb, b2)):
                sp.dma_start(dst[:], src).then_inc(s["ld_late"], 16)
            for e in range(2):
                sp.dma_start(w1_sb[:, e, :], w1T[e]).then_inc(ld_w[e], 16)
                sp.dma_start(w2_sb[:, e, :, :], w2T[e]).then_inc(ld_w[e], 16)
                sp.dma_start(b1_sb[:, e, :], b1T[e]).then_inc(ld_w[e], 16)
            with sp.Fori(0, E // 2 - 1) as i:
                for e in range(2):
                    nxt = sp.snap(i * 2 + (e + 2))
                    used = sp.snap(i * 4 + (2 * e + 2))
                    sp.wait_ge(s["y_ready"], used)
                    sp.dma_start(w1_sb[:, e, :], w1T[bass.ds(nxt, 1)].rearrange("o p n -> (o p) n")
                                 ).then_inc(ld_w[e], 16)
                    sp.dma_start(w2_sb[:, e, :, :],
                                 w2T[bass.ds(nxt, 1)].rearrange("o p c n -> (o p) c n")
                                 ).then_inc(ld_w[e], 16)
                    sp.dma_start(b1_sb[:, e, :], b1T[bass.ds(nxt, 1)].rearrange("o p n -> (o p) n")
                                 ).then_inc(ld_w[e], 16)
            for b in range(B):
                sp.wait_ge(s["fin_ready"], TB * (b + 1))
                sp.dma_start(out[:, b], fin[:, b]).then_inc(s["out_done"], 16)
            sp.wait_ge(s["out_done"], 16 * B)

        @block.tensor
        def _(pe):
            mm = nc.tensor.matmul

            def inc(ins, name):
                ins.then_inc(s[name], 1)

            pe.wait_ge(s["ld_attn"], 16 * N_ATTN)
            pe.wait_ge(s["wrep_ready"], 3)

            def projections(b):
                if b:
                    pe.wait_ge(s["acc_init"], b)
                xt = xT_sb[:, b, :]
                inc(mm(PS[:, 0, :], wfb[:, 0, :], xt, start=True, stop=True), "proj_ready")
                inc(mm(PS[:, 1, :], wfb[:, 1, :], xt, start=True, stop=True), "proj_ready")
                inc(mm(PS[0:DH, 2, :], gw1, xt, start=True, stop=True), "proj_ready")
                inc(mm(PS[:, 3, :], wqkv_sb[:, 1, :], xt, start=True, stop=True), "proj_ready")
                for t in range(TB):
                    last = mm(PS[:, 4, t * P:(t + 1) * P], xt[:, t * P:(t + 1) * P], wq, start=True, stop=True)
                inc(last, "proj_ready")
                pe.wait_ge(s["gh_ready"], b + 1)
                inc(mm(PS[:, 2, :], gw2_sb[:], gateh[:], start=True, stop=True), "proj_ready")
                pe.wait_ge(s["ksq_ready"], b + 1)
                inc(mm(PS[:, 5, :], headones, sq[:], start=True, stop=True), "ksum_ready")

            def replicated(b, n):
                if n >= 4:
                    pe.wait_ge(s["rep_used"], 16 * b + n - 3)
                elif n == 2:
                    pe.wait_ge(s["f_ready"], b + 1)
                    pe.wait_ge(s["beta_ready"], b + 1)
                inc(mm(PS[:, (6, 7, 0, 1)[n % 4], :], wrep[:, n // DH, n % DH, :], xT_sb[:, b, :],
                       start=True, stop=True), "rep_ready")

            def state_transposes(b, half):
                pe.wait_ge(s["kk_ready"], DH * b + 4 * (half + 1))
                for t in range(TB):
                    m = half * TB + t
                    if m == 0:
                        pe.wait_ge(s["gate_ready"], b + 1)
                        pe.wait_ge(s["kvec_ready"], b + 1)
                        pe.wait_ge(s["qn_ready"], b + 1)
                    if m >= 4:
                        pe.wait_ge(s["m_ready"], 8 * b + m - 3)
                    for jj in range(4):
                        last = nc.tensor.transpose(PS[:, 2 + m % 4, jj * P:(jj + 1) * P],
                                                   Akk[:, 4 * half + jj, t * P:(t + 1) * P], ident)
                    inc(last, "tr_ready")

            def recurrent_output(b):
                pe.wait_ge(s["solved"], b + 1)
                for t in range(TB):
                    last = nc.tensor.transpose(PS[:, 0, t * P:(t + 1) * P],
                                               xsol[:, t * P:(t + 1) * P], ident)
                inc(last, "qsT_ready")
                for j in range(DH):
                    pe.wait_ge(s["okv_ready"], DH * b + j + 1)
                    last = mm(PS[:, 1, :], sel[:, j, :], Akv[:, j, :], start=(j == 0), stop=(j == DH - 1))
                inc(last, "oT_ready")
                pe.wait_ge(s["ogsq_ready"], b + 1)
                inc(mm(PS[:, 2, :], headones, sq[:], start=True, stop=True), "ogms_ready")
                pe.wait_ge(s["attn_ready"], b + 1)
                for t in range(TB):
                    last = mm(PS[:, 3, t * P:(t + 1) * P], attn[:, t * P:(t + 1) * P], wo_sb[:],
                              start=True, stop=True)
                inc(last, "attny_ready")

            def cross_queries(b):
                pe.wait_ge(s["x1_ready"], TB * (b + 1))
                for t in range(TB):
                    last = nc.tensor.transpose(PS[:, 4, t * P:(t + 1) * P], x1[:, t, :], ident)
                inc(last, "x1T_ready")
                pe.wait_ge(s["x1T_sb"], b + 1)
                for g in range(2):
                    inc(mm(PS[0:64, 6 + g, :], xwq[:, g * 64:(g + 1) * 64], x1T[:], start=True, stop=True), "xq_ready")

            def score_maxima(b):
                pe.wait_ge(s["xq_sb"], 2 * (b + 1))
                for n in range(2 * TB):
                    t, g = divmod(n, 2)
                    if n >= 2:
                        pe.wait_ge(s["mx_ready"], 2 * TB * b + n - 1)
                    for k, (h0, nh) in enumerate(((0, 3), (3, 3), (6, 2))):
                        last = mm(PS[:, 3 * g + k, 0:nh * C], Qx[0:64, g, t * P:(t + 1) * P],
                                  Kb[0:64, b, g, h0:h0 + nh, :], start=True, stop=True)
                    inc(last, "ms_ready")
                pe.wait_ge(s["mx_ready"], 2 * TB * (b + 1))
                for g in range(2):
                    for t in range(TB):
                        last = mm(PS[0:72, 6 + g, t * P:(t + 1) * P], nmx[:, t, g, :], ident, start=True, stop=True)
                    inc(last, "nm_ready")

            def scores(b, r):
                g, st = divmod(r, 5)
                if r >= 2:
                    pe.wait_ge(s["p_ready"], 10 * b + r - 1)
                for k in range(2):
                    keys = Kr[:, b, g, 4 * k:4 * k + 4, :] if st == 0 else Kb[:, b, g, 2 * (st - 1) + k, 0:P]
                    last = mm(PS[:, 2 * (r % 2) + k, :], keys, Qx[:, g, :], start=True, stop=True)
                inc(last, "sc_ready")

            def values(b, r):
                g, st = divmod(r, 5)
                pe.wait_ge(s["p_ready"], 10 * b + r + 1)
                for k in range(2):
                    if st == 0:
                        qd = 2 * g + k
                        last = mm(PS[:, 4 + qd, :], Vr[:, b, qd, :, :], Pr[:, k, :], start=True, stop=False,
                                  skip_group_check=True)
                    else:
                        h = DH * g + 2 * (st - 1) + k
                        qd, a = divmod(h, 4)
                        last = mm(PS[32 * a:32 * a + 32, 4 + qd, :], Vm[:, b, h, :],
                                  Pm[:, (4 * g + st - 1) % 3, k, :], start=False, stop=True,
                                  tile_position=(0, 32 * a), skip_group_check=True)
                inc(last, "pv_done")

            def cross_output(b):
                for t in range(TB):
                    pe.wait_ge(s["ox_sb"], NQ * (b + 1))
                    for qd in range(NQ):
                        last = nc.tensor.transpose(PS[:, t, qd * P:(qd + 1) * P], Osb[:, qd, t * P:(t + 1) * P], ident)
                    inc(last, "xt_ready")
                pe.wait_ge(s["on_ready"], b + 1)
                for t in range(TB):
                    last = nc.tensor.transpose(
                        PS[:, 4, t * P:(t + 1) * P],
                        On[:, t * H:(t + 1) * H, :].rearrange("p h k -> p (h k)"), ident)
                inc(last, "onT_ready")
                pe.wait_ge(s["onT_sb"], b + 1)
                for t in range(TB):
                    last = mm(PS[:, 5, t * P:(t + 1) * P], OnT[:, t * P:(t + 1) * P], xwo, start=True, stop=True)
                inc(last, "xy_ready")

            def router(b):
                pe.wait_ge(s["x2_ready"], TB * (b + 1))
                for t in range(TB):
                    last = nc.tensor.transpose(PS[:, 6, t * P:(t + 1) * P], x2[:, b, t, :], ident)
                inc(last, "x2T_ready")
                pe.wait_ge(s["x2T_sb"], b + 1)
                for t in range(TB):
                    last = mm(PS[:, 7, t * E:(t + 1) * E], x2T[:, b, t * P:(t + 1) * P], rcomb[:], start=True, stop=True)
                inc(last, "lg_ready")
                pe.wait_ge(s["g_ready"], b + 1)
                for t in range(TB):
                    last = nc.tensor.transpose(PS[0:E, 0, t * P:(t + 1) * P], gates[:, b * TB + t, :], ident)
                inc(last, "gT_ready")
                pe.wait_ge(s["gT_sb"], b + 1)
                for t in range(TB):
                    last = mm(PS[:, 1, t * P:(t + 1) * P], gatesT[:, t * P:(t + 1) * P], b2_sb[:], start=True, stop=True)
                inc(last, "acc_in_ready")

            def cross_setup():
                pe.wait_ge(s["ld_late"], 16 * N_LATE)
                pe.wait_ge(s["keysq_ready"], 1)
                inc(mm(PS[:, 0, 0:E], onesq[:], keysq[:], start=True, stop=True), "key_ready")
                for g in range(2):
                    inc(mm(PS[0:64, 1 + g, 0:B * C], xwk[:, g * 64:(g + 1) * 64],
                           ctxT_sb[:].rearrange("p b c -> p (b c)"), start=True, stop=True), "kx_ready")
                pe.wait_ge(s["ctxR_ready"], 1)
                for b in range(B):
                    mm(PS[:, 3 + b, 0:P], ctxT_sb[:, b, 0:P], xwv, start=True, stop=True)
                    last = mm(PS[:, 5 + b, 0:P], ctxR[:, b, :, :], xwv, start=True, stop=True)
                inc(last, "vx_ready")
                pe.wait_ge(s["kx_sb"], 2)
                pe.wait_ge(s["v_ready"], 1)

            cross_setup()
            for b in range(B):
                projections(b)
                for n in range(DH):
                    replicated(b, n)
                state_transposes(b, 0)
                replicated(b, DH)
                replicated(b, DH + 1)
                state_transposes(b, 1)
                for n in range(DH + 2, 2 * DH):
                    replicated(b, n)
                recurrent_output(b)
                cross_queries(b)
                score_maxima(b)
                pe.wait_ge(s["nm_sb"], 2 * (b + 1))
                scores(b, 0)
                for r in range(10):
                    if r < 9:
                        scores(b, r + 1)
                    values(b, r)
                cross_output(b)
                router(b)

            pe.wait_ge(s["acc_init"], B)
            with pe.Fori(0, E // 2) as i:
                def up(u):
                    e, b = divmod(u, B)
                    if b == 0:
                        pe.wait_ge(ld_w[e], i * 48 + 48)
                    for c in range(FC):
                        if u:
                            pe.wait_ge(s["gelu_ready"], i * (4 * FC) + (FC * (u - 1) + c + 1))
                        inc(mm(PS[:, c, :], w1_sb[:, e, c * P:(c + 1) * P], x2T[:, b, :], start=True, stop=True),
                            "h_ready")

                def down(u):
                    e, b = divmod(u, B)
                    pe.wait_ge(s["gelu_ready"], i * (4 * FC) + FC * (u + 1))
                    if u >= 2:
                        pe.wait_ge(s["acc_done"], i * (4 * TB) + TB * (u - 1))
                    for t in range(TB):
                        for c in range(FC):
                            last = mm(PS[:, 4 + u % 2, t * P:(t + 1) * P], hid[:, u % 2, c, t * P:(t + 1) * P],
                                      w2_sb[:, e, c, :], start=(c == 0), stop=(c == FC - 1))
                    inc(last, "y_ready")

                up(0)
                for u in range(4):
                    if u < 3:
                        up(u + 1)
                    down(u)
                pe.wait_ge(s["acc_done"], i * (4 * TB) + 4 * TB)

        @block.scalar
        def _(act):
            A = nc.scalar.activation
            count = {}

            def step(ins, name="act_chain"):
                ins.then_inc(s[name], 1)
                count[name] = count.get(name, 0) + 1
                act.wait_ge(s[name], count[name])

            def rsqrt(dst, src, name, scale=1.0, eps=L2_EPS):
                step(A(dst, src, ACT.Ln, bias=eps_sb[:, 0:1] if eps == L2_EPS else eps_sb[:, 1:2], scale=scale))
                step(A(dst, dst, ACT.Exp, scale=-0.5), name)

            eps_sb = epst
            act.wait_ge(s["pool_set"], 1)
            act.wait_ge(s["ld_attn"], 16 * N_ATTN)
            nc.scalar.preload_act_table_set(LNEXP)
            step(A(softtmp[:], lamb_row, ACT.Abs))
            step(A(softtmp[:], softtmp[:], ACT.Exp, scale=-1.0))
            step(A(softtmp[:], softtmp[:], ACT.Ln, bias=1.0), "lamb_ln")
            act.wait_ge(s["ld_late"], 16 * N_LATE)
            step(A(keysq[:], keysrw_sb[:, 0, :], ACT.Square), "keysq_ready")
            for g in range(2):
                act.wait_ge(s["kx_ready"], g + 1)
                step(A(kx[:, g, :], PS[0:64, 1 + g, 0:B * C], ACT.Identity, bias=cols_sb[0:64, 4 + g:5 + g]), "kx_sb")

            for b in range(B):
                act.wait_ge(s["proj_ready"], 6 * b + 1)
                step(A(fgt[:], PS[:, 0, :], ACT.Sigmoid, bias=delta_col), "f_ready")
                act.wait_ge(s["proj_ready"], 6 * b + 2)
                step(A(beta[:], PS[:, 1, :], ACT.Sigmoid), "beta_ready")
                act.wait_ge(s["proj_ready"], 6 * b + 3)
                step(nc.scalar.copy(gateh[:], PS[0:DH, 2, :]), "gh_ready")
                act.wait_ge(s["proj_ready"], 6 * b + 4)
                step(A(sq[:], PS[:, 3, :], ACT.Square), "ksq_ready")
                act.wait_ge(s["proj_ready"], 6 * b + 5)
                step(A(qsq[:], PS[:, 4, :], ACT.Square), "qsq_ready")
                act.wait_ge(s["proj_ready"], 6 * b + 6)
                step(A(gateT[:], PS[:, 2, :], ACT.Sigmoid), "gate_ready")
                nc.scalar.preload_act_table_set(LNEXP)
                act.wait_ge(s["ksum_ready"], b + 1)
                rsqrt(kinv[:], PS[:, 5, :], "kinv_ready")
                act.wait_ge(s["qss_ready"], b + 1)
                rsqrt(qinv[:], qss[:], "qinv_ready")
                for m in range(2 * TB):
                    half, t = divmod(m, TB)
                    act.wait_ge(s["tr_ready"], 2 * TB * b + m + 1)
                    step(nc.scalar.copy(
                        M[:, :, 4 * half:4 * half + 4, t * H:(t + 1) * H].rearrange("p i j h -> p j h i"),
                        PS[:, 2 + m % 4, :].rearrange("p (j h i) -> p j h i", j=4, h=H)), "m_ready")
                act.wait_ge(s["og_ready"], b + 1)
                step(A(sq[:], og[:], ACT.Square), "ogsq_ready")
                act.wait_ge(s["ogms_ready"], b + 1)
                rsqrt(kinv[:], PS[:, 2, :], "ogr_ready", scale=1.0 / DH, eps=NORM_EPS)
                act.wait_ge(s["stats_ready"], 2 * b + 1)
                rsqrt(rstd[:], mv[:, :, 1], "rstd_ready", eps=NORM_EPS)
                act.wait_ge(s["x1T_ready"], b + 1)
                step(nc.scalar.copy(x1T[:], PS[:, 4, :]), "x1T_sb")
                for g in range(2):
                    act.wait_ge(s["xq_ready"], 2 * b + g + 1)
                    step(A(Qx[0:64, g, :], PS[0:64, 6 + g, :], ACT.Identity, bias=cols_sb[0:64, 2 + g:3 + g]), "xq_sb")
                for g in range(2):
                    act.wait_ge(s["nm_ready"], 2 * b + g + 1)
                    step(nc.scalar.copy(Qx[64:72, g, :], PS[64:72, 6 + g, :]), "nm_sb")
                for r in range(10):
                    g, st = divmod(r, 5)
                    act.wait_ge(s["sc_ready"], 10 * b + r + 1)
                    if st == 0:
                        dst = Pr[:, :, :]
                        if r:
                            act.wait_ge(s["pv_done"], 10 * b + 1)
                    else:
                        m = 4 * g + st - 1
                        dst = Pm[:, m % 3, :, :]
                        if m >= 3:
                            act.wait_ge(s["pv_done"], 10 * b + (m - 3) + 2 + (1 if m - 3 >= 4 else 0))
                    step(A(dst, PS[:, 2 * (r % 2):2 * (r % 2) + 2, :], ACT.Exp, scale=SM_SCALE), "p_ready")
                for qd in range(NQ):
                    act.wait_ge(s["pv_done"], 10 * b + (3 if qd == 0 else 5 if qd == 1 else 8 if qd == 2 else 10))
                    step(nc.scalar.copy(Osb[:, qd, :], PS[:, 4 + qd, :]), "ox_sb")
                act.wait_ge(s["onT_ready"], b + 1)
                step(nc.scalar.copy(OnT[:], PS[:, 4, :]), "onT_sb")
                act.wait_ge(s["stats_ready"], 2 * b + 2)
                rsqrt(rstd[:], mv[:, :, 1], "rstd_ready", eps=NORM_EPS)
                act.wait_ge(s["x2_ready"], TB * (b + 1))
                for t in range(TB):
                    step(A(sq[:, t * P:(t + 1) * P], x2[:, b, t, :], ACT.Square, accum_out=xsq[:, t:t + 1]), "xsq_ready")
                act.wait_ge(s["x2T_ready"], b + 1)
                step(nc.scalar.copy(x2T[:, b, :], PS[:, 6, :]), "x2T_sb")
                act.wait_ge(s["w4_diff"], b + 1)
                step(A(w4[:], w4[:], ACT.Exp), "w4_ready")
                act.wait_ge(s["gT_ready"], b + 1)
                step(nc.scalar.copy(gatesT[:], PS[0:E, 0, :]), "gT_sb")

            nc.scalar.preload_act_table(ACT.Gelu)
            with act.Fori(0, E // 2) as i:
                for u in range(4):
                    e, b = divmod(u, B)
                    for c in range(FC):
                        act.wait_ge(s["h_ready"], i * (4 * FC) + (FC * u + c + 1))
                        if c == 0 and u >= 2:
                            act.wait_ge(s["y_ready"], i * 4 + (u - 1))
                        A(hid[:, u % 2, c, :], PS[:, c, :], ACT.Gelu, bias=b1_sb[:, e, c:c + 1]).then_inc(
                            s["gelu_ready"], 1)
                act.wait_ge(s["y_ready"], i * 4 + 4)
            for b in range(B):
                act.wait_ge(s["stats_ready"], 2 * B + b + 1)
                rsqrt(rstd[:], mv[:, :, 1], "rstd_ready", eps=NORM_EPS)

        @block.gpsimd
        def _(pool):
            count = [0]
            nc.gpsimd.memset(epst[:, 0:1], L2_EPS)
            nc.gpsimd.memset(epst[:, 1:2], NORM_EPS)
            nc.gpsimd.memset(onesq[:], 1.0)
            nc.gpsimd.memset(Kr[:], 0.0)
            nc.gpsimd.memset(ctxR[:], 0.0)
            nc.gpsimd.memset(Vr[:], 0.0)
            nc.gpsimd.memset(nmx[:], 0.0)
            nc.gpsimd.memset(Vm[:], 0.0).then_inc(s["pool_set"], 1)

        @block.vector
        def _(dve):
            V = nc.vector
            count = {}

            def step(ins, name="dve_chain"):
                ins.then_inc(s[name], 1)
                count[name] = count.get(name, 0) + 1
                dve.wait_ge(s[name], count[name])

            def tt(o, a, c, op, name="dve_chain"):
                step(V.tensor_tensor(o, a, c, op), name)

            def layernorm(dst, b, signal):
                for t in range(TB):
                    step(V.bn_stats(stats[:, t, :], res[:, t, :]))
                for t in range(TB):
                    last = V.bn_aggr(mv[:, t, :], stats[:, t, :])
                    if t < TB - 1:
                        step(last)
                step(last, "stats_ready")
                dve.wait_ge(s["rstd_ready"], count["stats_ready"])
                for t in range(TB):
                    step(V.tensor_scalar(dst[:, t, :], res[:, t, :], mv[:, t, 0:1], rstd[:, t:t + 1],
                                         ALU.subtract, ALU.mult), signal)

            dve.wait_ge(s["pool_set"], 1)
            dve.wait_ge(s["ld_attn"], 16 * N_ATTN)
            for k in range(2):
                step(V.tensor_copy(wrep[:, k, :, :].rearrange("p j (h i) -> p j h i", h=H),
                                   bc(wqkv_sb[:, 1 + k, :].rearrange("p (h j) -> p j h", h=H), 3, DH)), "wrep_ready")
            step(V.tensor_copy(wfb[:].rearrange("p k (h i) -> p (k h) i", h=H), bc(wsmall_sb[:, 0:2 * H], 2, DH)),
                 "wrep_ready")
            dve.wait_ge(s["lamb_ln"], 1)
            step(V.scalar_tensor_tensor(lamb[:], lamb_row, 0.0, softtmp[:], ALU.max, ALU.add))
            step(V.tensor_scalar(lamb[:], lamb[:], LAMBDA_LOWER, None, ALU.add))
            step(V.tensor_copy(ctxR[:, :, :, 0:CR], bc(ctxT_sb[:, :, P:C], 2, 4)), "ctxR_ready")
            dve.wait_ge(s["ld_late"], 16 * N_LATE)
            step(V.scalar_tensor_tensor(rcomb[:], keysrw_sb[:, 0, :], 2.0, keysrw_sb[:, 1, :], ALU.mult, ALU.add))
            dve.wait_ge(s["key_ready"], 1)
            tt(cE[:], rb_row, PS[:, 0, 0:E], ALU.subtract)
            dve.wait_ge(s["kx_sb"], 2)
            for b in range(B):
                for g in range(2):
                    tt(Kb[0:64, b, g, :, :], bc(kx[:, g, b * C:(b + 1) * C], 1, DH), bc(hmask[0:64, :], 2, C), ALU.mult)
                    step(V.tensor_copy(Kb[64:72, b, g, :, :], bc(hmask[64:72, :], 2, C)))
                    step(V.tensor_copy(Kr[:, b, g, :, 0:CR], Kb[:, b, g, :, P:C]), "kb_ready")
            dve.wait_ge(s["vx_ready"], 1)
            for b in range(B):
                tt(Vm[:, b, :, 0:DH], PS[:, 3 + b, 0:P].rearrange("p (h k) -> p h k", h=H),
                   bv_row.rearrange("p (h k) -> p h k", h=H), ALU.add)
                step(V.memset(Vm[:, b, :, DH:DH + 1], 1.0))
                for a in range(4):
                    rows = slice(32 * a, 32 * a + CR)
                    tt(Vr[rows, b, :, a, 0:DH],
                       PS[rows, 5 + b, 0:P].rearrange("p (q a k) -> p q a k", q=NQ, a=4)[:, :, a, :],
                       bv_row[rows, :].rearrange("p (q a k) -> p q a k", q=NQ, a=4)[:, :, a, :], ALU.add)
                    last = V.memset(Vr[rows, b, :, a, DH:DH + 1], 1.0)
                    if (b, a) != (B - 1, 3):
                        step(last)
            step(last, "v_ready")

            for b in range(B):
                dve.wait_ge(s["proj_ready"], 6 * b + 4)
                dve.wait_ge(s["kinv_ready"], b + 1)
                tt(kbeta[:], PS[:, 3, :], kinv[:], ALU.mult)
                dve.wait_ge(s["beta_ready"], b + 1)
                tt(kbeta[:], kbeta[:], beta[:], ALU.mult)
                tt(kc[:], kbeta[:], kinv[:], ALU.mult, "kvec_ready")
                dve.wait_ge(s["qsq_ready"], b + 1)
                step(V.tensor_reduce(qss[:], qsq[:].rearrange("p (g i) -> p g i", i=DH), AX.X, ALU.add), "qss_ready")
                dve.wait_ge(s["f_ready"], b + 1)
                for n in range(2 * DH):
                    j = n % DH
                    dve.wait_ge(s["rep_ready"], 16 * b + n + 1)
                    tt(prod[:], (kc if n < DH else kbeta)[:], PS[:, (6, 7, 0, 1)[n % 4], :], ALU.mult, "rep_used")
                    step(V.tensor_tensor_scan((Akk if n < DH else Akv)[:, j, :], fgt[:], prod[:], 0.0,
                                              ALU.mult, ALU.add), "kk_ready" if n < DH else "dve_chain")
                    if n == 0:
                        dve.wait_ge(s["qinv_ready"], b + 1)
                        tt(M[:, :, DH, :].rearrange("p i g -> p g i"),
                           PS[:, 4, :].rearrange("p (g i) -> p g i", i=DH), bc(qinv[:], 2, DH), ALU.mult, "qn_ready")
                dve.wait_ge(s["m_ready"], 8 * (b + 1))
                Md = M[:].rearrange("p i j g -> p (i j) g")[:, 0:DH * (DH + 1):DH + 2, :].rearrange(
                    "p i (t h) -> p i t h", t=TB)
                tt(Md, Md, bc(lamb[:].rearrange("p (h i) -> p i h", h=H), 2, TB), ALU.add)
                for k in range(DH):
                    n = DH - 1 - k
                    step(V.reciprocal(rpiv[:], M[:, k, k, :]))
                    tt(U[:, k, k + 1:, :], M[:, k, k + 1:, :], bc(rpiv[:], 1, n + 1), ALU.mult)
                    if n:
                        upd = tmp[:, 0:n, 0:n + 1, :]
                        tt(upd, bc(M[:, k, k + 1:DH, :], 2, n + 1), bc(U[:, k, k + 1:, :], 1, n), ALU.mult)
                        tt(M[:, k + 1:, k + 1:, :], M[:, k + 1:, k + 1:, :], upd, ALU.subtract)
                for j in range(DH - 1, 0, -1):
                    tt(tmp[:, 0:j, 0, :], U[:, 0:j, j, :], bc(U[:, j, DH, :], 1, j), ALU.mult)
                    tt(U[:, 0:j, DH, :], U[:, 0:j, DH, :], tmp[:, 0:j, 0, :], ALU.subtract)
                step(V.tensor_copy(xsol[:].rearrange("p (g i) -> p i g", i=DH), U[:, :, DH, :]), "solved")
                dve.wait_ge(s["qsT_ready"], b + 1)
                for j in range(DH):
                    tt(Akv[:, j, :], Akv[:, j, :], PS[:, 0, :], ALU.mult, "okv_ready")
                dve.wait_ge(s["oT_ready"], b + 1)
                dve.wait_ge(s["gate_ready"], b + 1)
                tt(og[:], PS[:, 1, :], gateT[:], ALU.mult, "og_ready")
                dve.wait_ge(s["ogr_ready"], b + 1)
                step(V.scalar_tensor_tensor(attn[:], og[:], normw_col, kinv[:], ALU.mult, ALU.mult), "attn_ready")
                dve.wait_ge(s["attny_ready"], b + 1)
                tt(res[:].rearrange("p t d -> p (t d)"), x_sb[:, b].rearrange("p t d -> p (t d)"), PS[:, 3, :], ALU.add)
                layernorm(x1, b, "x1_ready")
                tt(x1b[:], x1[:], bc(bo_row, 1, TB), ALU.add)
                for n in range(2 * TB):
                    t, g = divmod(n, 2)
                    dve.wait_ge(s["ms_ready"], 2 * TB * b + n + 1)
                    step(V.tensor_reduce(nmx[:, t, g, 64:70].rearrange("p (k h) -> p k h", k=2),
                                         PS[:, 3 * g:3 * g + 2, 0:3 * C].rearrange("p k (h c) -> p k h c", h=3),
                                         AX.X, ALU.max, negate=True))
                    step(V.tensor_reduce(nmx[:, t, g, 70:72],
                                         PS[:, 3 * g + 2, 0:2 * C].rearrange("p (h c) -> p h c", h=2),
                                         AX.X, ALU.max, negate=True), "mx_ready")
                dve.wait_ge(s["xt_ready"], TB * (b + 1))
                T = PS[:, 0:TB, :].rearrange("p t (h w) -> p (t h) w", w=32)
                step(V.reciprocal(rden[:], T[:, :, DH]))
                tt(On[:], T[:, :, 0:DH], bc(rden[:], 2, DH), ALU.mult, "on_ready")
                dve.wait_ge(s["xy_ready"], b + 1)
                tt(res[:].rearrange("p t d -> p (t d)"), x1b[:].rearrange("p t d -> p (t d)"), PS[:, 5, :], ALU.add)
                layernorm(x2[:, b], b, "x2_ready")
                dve.wait_ge(s["lg_ready"], b + 1)
                tt(logit[:], PS[:, 7, 0:TB * E].rearrange("p (t e) -> p t e", t=TB), bc(cE[:], 1, TB), ALU.add)
                dve.wait_ge(s["xsq_ready"], TB * (b + 1))
                tt(logit[:], logit[:], bc(xsq[:], 2, E), ALU.subtract)
                for t in range(TB):
                    step(V.max(top8[:, t, :], logit[:, t, :]))
                    step(V.max_index(idx8[:, t, :], top8[:, t, :], logit[:, t, :]))
                step(V.tensor_copy(idx4[:], idx8[:, :, 0:TOPK]))
                tt(w4[:], top8[:, :, 0:TOPK], bc(top8[:, :, 0], 2, TOPK), ALU.subtract, "w4_diff")
                tt(oneh[:], bc(iota, 1, TB * TOPK), bc(idx4[:].rearrange("p t r -> p (t r)"), 2, E), ALU.is_equal)
                dve.wait_ge(s["w4_ready"], b + 1)
                step(V.tensor_reduce(wsum[:], w4[:], AX.X, ALU.add))
                step(V.reciprocal(wsum[:], wsum[:]))
                tt(w4[:], w4[:], bc(wsum[:], 2, TOPK), ALU.mult)
                tt(oneh[:], oneh[:], bc(w4[:].rearrange("p t r -> p (t r)"), 2, E), ALU.mult)
                step(V.tensor_reduce(gates[:, b * TB:(b + 1) * TB, :],
                                     oneh[:].rearrange("p (t r) e -> p t e r", t=TB), AX.X, ALU.add), "g_ready")
                dve.wait_ge(s["acc_in_ready"], b + 1)
                tt(acc[:, b].rearrange("p t d -> p (t d)"), x2[:, b].rearrange("p t d -> p (t d)"), PS[:, 1, :],
                   ALU.add, "acc_init")

            with dve.Fori(0, E // 2) as i:
                for u in range(4):
                    e, b = divmod(u, B)
                    if b == 0:
                        V.tensor_copy(gslot[:, e, :], gates[:, :, bass.ds(i * 2 + e, 1)].rearrange("p t o -> p (t o)")
                                      ).then_inc(s["gslot_ready"], 1)
                        dve.wait_ge(s["gslot_ready"], i * 2 + (e + 1))
                    dve.wait_ge(s["y_ready"], i * 4 + (u + 1))
                    for t in range(TB):
                        V.scalar_tensor_tensor(acc[:, b, t, :], PS[:, 4 + u % 2, t * P:(t + 1) * P],
                                               gslot[:, e, b * TB + t:b * TB + t + 1], acc[:, b, t, :],
                                               ALU.mult, ALU.add).then_inc(s["acc_done"], 1)
                dve.wait_ge(s["acc_done"], i * (4 * TB) + 4 * TB)
            for b in range(B):
                step(V.tensor_copy(res[:], acc[:, b]))
                layernorm(fin[:, b], b, "fin_ready")


_OUTS = [((B, S, D), "float32")]


def kernel(**inputs):
    import numpy as np
    import concourse.bacc as bacc
    from concourse.bass_utils import run_bass_kernel_spmd

    a = {k: np.asarray(v) for k, v in inputs.items()}

    def w(name):
        return a["L0_" + name]

    def token_blocks(v):
        return v.reshape(B, TB, P, D).transpose(2, 0, 1, 3)

    cols = np.zeros((P, 6), np.float32)
    cols[:, 0] = np.repeat(w("attn_delta"), DH)
    cols[:, 1] = w("attn_norm_weight")
    cols[0:64, 2:4] = w("xattn_bq").reshape(2, 64).T
    cols[0:64, 4:6] = w("xattn_bk").reshape(2, 64).T
    r = np.arange(P)
    consts = np.zeros((P, 2 * P + DH * P + DH + E), np.float32)
    consts[:, 0:P] = np.eye(P)
    consts[:, P:2 * P] = r[:, None] // DH == r[None, :] // DH
    for j in range(DH):
        consts[:, 2 * P + j * P:2 * P + (j + 1) * P] = (r[:, None] // DH == r[None, :] // DH) & (r[None, :] % DH == j)
    m = consts[:, 2 * P + DH * P:]
    m[0:64, 0:DH] = r[0:64, None] // DH == np.arange(DH)
    m[64:72, 0:DH] = np.eye(DH)
    m[:, DH:] = np.arange(E)
    arrays = {
        "xTok": token_blocks(a["x"]),
        "xT": a["x"].transpose(2, 0, 1),
        "ctxT": a["ctx_1024"].transpose(2, 0, 1),
        "wqkv": np.stack([w("attn_Wq"), w("attn_Wk"), w("attn_Wv")], 1),
        "wsmall": np.concatenate([w("attn_Wf"), w("attn_Wbet"), w("attn_gate_w1")], 1),
        "gw2": w("attn_gate_w2"),
        "wo": w("attn_Wo"),
        "cols": cols,
        "lamb": w("attn_lamb_params"), "bv": w("xattn_bv"), "bo": w("xattn_bo"), "rb": w("ffn_rb"),
        "xw": np.stack([w("xattn_Wq"), w("xattn_Wk"), w("xattn_Wv"), w("xattn_Wo")], 1),
        "keysrw": np.stack([w("ffn_keys").T, w("ffn_rw").T], 1),
        "b2": w("ffn_b2"),
        "w1T": w("ffn_w1").transpose(0, 2, 1),
        "w2T": w("ffn_w2").transpose(0, 2, 1).reshape(E, FC, P, D).transpose(0, 2, 1, 3),
        "b1T": w("ffn_b1").reshape(E, FC, P).transpose(0, 2, 1),
        "consts": consts,
    }
    arrays = {k: np.ascontiguousarray(v) for k, v in arrays.items()}
    nc = bacc.Bacc("TRN2", target_bir_lowering=False, num_devices=1)
    t = {k: nc.dram_tensor(f"in_{k}", v.shape, F32, kind="ExternalInput").ap() for k, v in arrays.items()}
    out = nc.dram_tensor("out", (B, S, D), F32, kind="ExternalOutput").ap()
    rows = [t.pop(k).rearrange("(o n) -> o n", o=1).broadcast_to((P, n))
            for k, n in (("lamb", D), ("bv", D), ("bo", D), ("rb", E))]
    decoder_layer(nc, rowsb=rows, out=out.rearrange("b (t p) d -> p b t d", p=P), **t)
    r = run_bass_kernel_spmd(nc, [{f"in_{k}": v for k, v in arrays.items()}], core_ids=[0])
    return r.results[0]["out"]
```

```python
from contextlib import ExitStack

import concourse.bass as bass
from concourse import mybir

F32 = mybir.dt.float32
F32R = mybir.dt.float32r
U32 = mybir.dt.uint32
ALU = mybir.AluOpType
ACT = mybir.ActivationFunctionType
AX = mybir.AxisListType

P = 128
B, S, D = 2, 512, 128
H, DH = 16, 8
TB = S // P
G = TB * H
C = 154
CR = C - P
NQ = H // 4
E, F = 16, 512
FC = F // P
TOPK = 4
LAMBDA_LOWER = 0.25
L2_EPS = 1e-6
NORM_EPS = 1e-5
SM_SCALE = DH ** -0.5
LNEXP = "natural_log_exp_and_others"


def bc(ap, axis, n):
    v = ap.unsqueeze(axis)
    shape = list(v.shape)
    shape[axis] = n
    return v.broadcast_to(tuple(shape))


def decoder_layer(nc, xTok, xT, ctxT, wqkv, wsmall, gw2, wo, cols, rowsb, xw, keysrw, b2, w1T, w2T, b1T, consts, out):
    ctx = ExitStack()
    with ctx:
        def sb(name, shape, dt=F32):
            return ctx.enter_context(nc.sbuf_tensor(name, shape, dt))

        def sem(name):
            return ctx.enter_context(nc.semaphore(name))

        def f(ap):
            return ap.bitcast(F32)

        PS = ctx.enter_context(nc.psum_tensor("PS", [P, 8, 512], F32))

        epst = sb("epst", [P, 2])
        x_sb = sb("x_sb", [P, B, TB, D])
        xT_sb = sb("xT_sb", [P, B, S])
        ctxT_sb = sb("ctxT_sb", [P, B, C])
        wqkv_sb = sb("wqkv_sb", [P, 3, D])
        wsmall_sb = sb("wsmall_sb", [P, 2 * H + DH])
        gw2_sb = sb("gw2_sb", [DH, D])
        wo_sb = sb("wo_sb", [P, D])
        cols_sb = sb("cols_sb", [P, 3 + 2 * NQ])
        rows_sb = sb("rows_sb", [P, 3 * D + E])
        xw_sb = sb("xw_sb", [P, 4, D])
        keysrw_sb = sb("keysrw_sb", [P, 2, E])
        b2_sb = sb("b2_sb", [E, D])
        const_sb = sb("const_sb", [P, 2 * P + DH * P + NQ * 4 + E])
        delta_col, normw_col, lowneg_col = (cols_sb[:, i:i + 1] for i in range(3))
        lamb_row, bv_row, bo_row = (rows_sb[:, i * D:(i + 1) * D] for i in range(3))
        rb_row = rows_sb[:, 3 * D:3 * D + E]
        ident = const_sb[:, 0:P]
        headones = const_sb[:, P:2 * P]
        sel = const_sb[:, 2 * P:2 * P + DH * P].rearrange("p (j n) -> p j n", j=DH)
        hmask = const_sb[:, 2 * P + DH * P:2 * P + DH * P + NQ * 4].rearrange("p (q a) -> p q a", q=NQ)
        iota = const_sb[:, 2 * P + DH * P + NQ * 4:]
        wq = wqkv_sb[:, 0, :]
        gw1 = wsmall_sb[:, 2 * H:2 * H + DH]
        xwq, xwk, xwv, xwo = (xw_sb[:, i, :] for i in range(4))

        wrep = sb("wrep", [P, 2, DH, D])
        wfb = sb("wfb", [P, 2, D])
        lamb = sb("lamb", [P, D])
        onesq = sb("onesq", [P, P])
        rcomb = sb("rcomb", [P, E])
        rcH = sb("rcH", [P, E], F32R)
        rcL = sb("rcL", [P, E], F32R)
        keysq = sb("keysq", [P, E])
        cE = sb("cE", [P, E])
        w3 = sb("w3", [P, 2, NQ, 3, 32])
        KS = sb("KS", [P, B, NQ, 4, C], F32R)
        Kr = sb("Kr", [P, B, NQ, 4, 32], F32R)
        Vm = sb("Vm", [P, B, H, 32])
        Vr = sb("Vr", [P, B, NQ, 4, 32])
        nmx = sb("nmx", [P, TB, P])

        hid = sb("hid", [P, 2, FC, S])
        sq, qsq, beta, kinv, qtok, kbeta, prod, gateh = (hid[:, i // FC, i % FC, :] for i in range(2 * FC))
        gateh = gateh[0:DH, :]
        fgt = sb("fgt", [P, S])
        gateT = sb("gateT", [P, B, S])
        kc = sb("kc", [P, S])
        qss = sb("qss", [P, G])
        qinv = sb("qinv", [P, G])
        Akk = sb("Akk", [P, DH, S])
        Akv = sb("Akv", [P, DH, S])
        M = sb("M", [P, DH, DH + 1, G])
        U = Akk[:].rearrange("p k (j g) -> p k j g", g=G)
        tmp = sb("tmp", [P, 24 * G])
        rpiv = sb("rpiv", [P, G])
        xsol = sb("xsol", [P, S])
        og = sb("og", [P, S])
        osq = sb("osq", [P, S])
        orr = sb("orr", [P, S])
        attn = osq

        res = sb("res", [P, TB, D])
        stats = sb("stats", [P, TB, 6])
        mv = sb("mv", [P, TB, 2])
        rstd = sb("rstd", [P, TB])
        x1b = res[:]
        x1 = og[:].rearrange("p (t d) -> p t d", t=TB)
        x1T = xsol
        QS = sb("QS", [P, NQ, S], F32R)
        Pt = sb("Pt", [P, 4, S])
        mh = Pt[:, 0, :].bitcast(F32R)
        Osb = sb("Osb", [P, NQ, S])
        rden = sb("rden", [P, TB * H])
        On = osq[:].rearrange("p (t k) -> p t k", k=DH)
        OnT = orr

        x2 = sb("x2", [P, B, TB, D])
        acc = x2
        x2H = sb("x2H", [P, B, S], F32R)
        x2L = sb("x2L", [P, B, S], F32R)
        xsq = sb("xsq", [P, TB])
        logit = sb("logit", [P, TB, E])
        top8 = sb("top8", [P, TB, 8])
        idx8 = sb("idx8", [P, TB, 8], U32)
        idx4 = sb("idx4", [P, TB, TOPK])
        w4 = sb("w4", [P, TB, TOPK])
        wsum = sb("wsum", [P, TB])
        oneh = sb("oneh", [P, TB * TOPK, E])
        gates = sb("gates", [P, B * TB, E])
        gatesT = xsol[0:E, :]
        gslot = sb("gslot", [P, 2, TB])
        w1H = sb("w1H", [P, 2, F], F32R)
        w1L = sb("w1L", [P, 2, F], F32R)
        w1_sb = wrep[:, 0, :, :].rearrange("p j n -> p (j n)").rearrange("p (k n) -> p k n", k=2)
        w2_sb = wrep[:, 1, :, :].rearrange("p j n -> p (j n)").rearrange("p (k c n) -> p k c n", k=2, c=FC)
        b1_sb = sb("b1_sb", [P, 2, FC])
        fin = x_sb
        scratch = Pt[:].rearrange("p r s -> p (r s)")
        kx = scratch[:, 0:NQ * B * C].rearrange("p (q n) -> p q n", q=NQ)
        vx = scratch[:, NQ * B * C:NQ * B * C + 2 * B * D].rearrange("p (k b n) -> p k b n", k=2, b=B)
        kE = scratch[:, 4 * S - E:]
        scratch = Osb[:].rearrange("p q s -> p (q s)")
        kxS = scratch[0:96, 0:NQ * B * C].bitcast(F32R).rearrange("p (q n) -> p q n", q=NQ)
        ctxR = scratch[:, NQ * B * C:NQ * B * C + B * 4 * 32].rearrange("p (b a n) -> p b a n", b=B, a=4)
        softtmp = scratch[:, 4 * S - D:]

        names = """ld_first ld_attn ld_late kk_free pool_set wrepv_ready w3_ready ctxR_ready lamb_abs lamb_ln lamb_ready wrep_ready
        k_ready q_ready zb_ready zf_ready gh_ready g2_ready ksum_ready ksq_ready kcp_ready ghc_ready beta_ready
        f_ready gate_ready qsq_ready qcp_ready kinv_ready qinv_ready kvec_ready qss_ready qn_ready
        rep_ready rep_used kk_ready tr_ready m_ready solved qsT_ready okv_ready oT_ready og_ready
        ogsq_ready ogms_ready ogr_ready attn_ready attny_ready stats_ready rstd_ready x1_ready x1T_ready x1T_sb
        xq_ready qh_ready ql_ready ms_ready mx_ready nmx_ready nm_ready mh_ready qm_ready sc_ready p_ready pv_done
        ox_sb xt_ready on_ready onT_ready onT_sb xy_ready x2_ready x2T_ready x2H_ready x2L_ready lg_ready xsq_ready
        w4_diff w4_ready g_ready gT_ready gT_sb acc_in_ready acc_init keysq_ready key_ready kE_sb kx_ready kx_sb
        vx_ready vx_sb rc_ready ks_ready v_ready cE_ready ws_ready gslot_ready
        dve_chain act_chain pool_chain h_ready gelu_ready y_ready acc_done out_done fin_ready"""
        s = {n: sem(n) for n in names.split()}
        ld_w1 = [sem(f"ld_w1_{i}") for i in range(2)]
        ld_w2 = [sem(f"ld_w2_{i}") for i in range(2)]
        wh_ready = [sem(f"wh_ready_{i}") for i in range(2)]

        block = ctx.enter_context(nc.Block())
        N_FIRST, N_ATTN, N_LATE = 5, 10, 6

        FRONT = (["q", "k", "zb", "zf", "ksum", "gh", "g2"] + [("rep", n) for n in range(DH + 2)]
                 + [("tr", m) for m in range(4)] + [("rep", DH + 2), ("rep", DH + 3)]
                 + [("tr", m) for m in range(4, 8)] + [("rep", n) for n in range(DH + 4, 2 * DH)])
        AT = {item: n for n, item in enumerate(FRONT)}

        def front_bank(item):
            return AT[item] % 4

        def front_read(item, b):
            if isinstance(item, tuple):
                kind, n = item
                return ("rep_used", 16 * b + n + 1) if kind == "rep" else ("m_ready", 8 * b + n + 1)
            return {"q": "qcp_ready", "k": "kcp_ready", "zb": "beta_ready", "zf": "f_ready", "ksum": "kinv_ready",
                    "gh": "ghc_ready", "g2": "gate_ready"}[item], b + 1

        def h_bank(b, n):
            return n % 3 if b == 0 else n % 4

        def y_bank(b, u):
            return 3 if b == 0 else 4 + u % 2

        @block.sync
        def _(sp):
            for n, (dst, src) in enumerate((
                    (xT_sb, xT), (wqkv_sb, wqkv), (wsmall_sb, wsmall), (cols_sb, cols), (const_sb, consts),
                    (gw2_sb, gw2), (rows_sb[:, 0:D], rowsb[0]), (ctxT_sb, ctxT), (x_sb, xTok), (wo_sb, wo))):
                sp.dma_start(dst[:], src).then_inc(s["ld_first" if n < N_FIRST else "ld_attn"], 16)
            for dst, src in ((rows_sb[:, D:2 * D], rowsb[1]), (rows_sb[:, 2 * D:3 * D], rowsb[2]),
                             (rows_sb[:, 3 * D:], rowsb[3]), (xw_sb, xw), (keysrw_sb, keysrw), (b2_sb, b2)):
                sp.dma_start(dst[:], src).then_inc(s["ld_late"], 16)

            def weights(k, e, done=None):
                def of(t, names):
                    return t[e] if isinstance(e, int) else t[bass.ds(e, 1)].rearrange(f"o p {names} -> (o p) {names}")
                if done is not None:
                    sp.wait_ge(s["ws_ready"], done)
                sp.dma_start(w1_sb[:, k, :], of(w1T, "n")).then_inc(ld_w1[k], 16)
                if done is not None:
                    sp.wait_ge(s["y_ready"], done)
                sp.dma_start(w2_sb[:, k, :, :], of(w2T, "c n")).then_inc(ld_w2[k], 16)
                sp.dma_start(b1_sb[:, k, :], of(b1T, "n")).then_inc(ld_w2[k], 16)

            sp.wait_ge(s["rep_used"], 32)
            for k in range(2):
                weights(k, k)
            for b in range(B):
                first = 2 if b == 0 else 0
                with sp.Fori(0, (E - first) // 2) as i:
                    for k in range(2):
                        weights(k, sp.snap(i * 2 + (first + k)), sp.snap(i * 2 + (E * b + first + k - 1)))
            for b in range(B):
                sp.wait_ge(s["fin_ready"], TB * (b + 1))
                sp.dma_start(out[:, b], fin[:, b]).then_inc(s["out_done"], 16)
            sp.wait_ge(s["out_done"], 16 * B)

        @block.tensor
        def _(pe):
            mm = nc.tensor.matmul

            def inc(ins, name):
                ins.then_inc(s[name], 1)

            def front(b, item):
                n = AT[item]
                bank = n % 4
                before = [m for m in range(len(FRONT)) if m % 4 == bank and (m < n)]
                if before:
                    name, value = front_read(FRONT[before[-1]], b)
                    pe.wait_ge(s[name], value)
                elif b:
                    last = [m for m in range(len(FRONT)) if m % 4 == bank][-1]
                    name, value = front_read(FRONT[last], b - 1)
                    pe.wait_ge(s[name], value)
                xt = xT_sb[:, b, :]
                o = PS[:, bank, :]
                if item == "q":
                    for t in range(TB):
                        last = mm(o[:, t * P:(t + 1) * P], xt[:, t * P:(t + 1) * P], wq, start=True, stop=True)
                    inc(last, "q_ready")
                elif item == "k":
                    inc(mm(o, wqkv_sb[:, 1, :], xt, start=True, stop=True), "k_ready")
                elif item == "zb":
                    inc(mm(o, wfb[:, 1, :], xt, start=True, stop=True), "zb_ready")
                elif item == "zf":
                    inc(mm(o, wfb[:, 0, :], xt, start=True, stop=True), "zf_ready")
                elif item == "ksum":
                    pe.wait_ge(s["ksq_ready"], b + 1)
                    inc(mm(o, headones, sq, start=True, stop=True), "ksum_ready")
                elif item == "gh":
                    inc(mm(o[0:DH, :], gw1, xt, start=True, stop=True), "gh_ready")
                elif item == "g2":
                    pe.wait_ge(s["ghc_ready"], b + 1)
                    inc(mm(o, gw2_sb[:], gateh, start=True, stop=True), "g2_ready")
                elif item[0] == "rep":
                    kv, j = divmod(item[1], DH)
                    if (b, item) == (0, ("rep", DH)):
                        pe.wait_ge(s["wrepv_ready"], 1)
                    inc(mm(o, wrep[:, kv, j, :], xt, start=True, stop=True), "rep_ready")
                else:
                    half, t = divmod(item[1], TB)
                    pe.wait_ge(s["kk_ready"], DH * b + 4 * (half + 1))
                    for jj in range(4):
                        last = nc.tensor.transpose(o[:, jj * P:(jj + 1) * P],
                                                   Akk[:, 4 * half + jj, t * P:(t + 1) * P], ident)
                    inc(last, "tr_ready")

            def solutions(b):
                pe.wait_ge(s["solved"], b + 1)
                for t in range(TB):
                    last = nc.tensor.transpose(PS[:, 4, t * P:(t + 1) * P], xsol[:, t * P:(t + 1) * P], ident)
                inc(last, "qsT_ready")

            def head_outputs(b):
                for j in range(DH):
                    pe.wait_ge(s["okv_ready"], DH * b + j + 1)
                    last = mm(PS[:, 5, :], sel[:, j, :], Akv[:, j, :], start=(j == 0), stop=(j == DH - 1))
                inc(last, "oT_ready")

            def head_squares(b):
                pe.wait_ge(s["ogsq_ready"], b + 1)
                inc(mm(PS[:, 6, :], headones, osq[:], start=True, stop=True), "ogms_ready")

            def attn_projection(b):
                pe.wait_ge(s["attn_ready"], b + 1)
                for t in range(TB):
                    last = mm(PS[:, 7, t * P:(t + 1) * P], attn[:, t * P:(t + 1) * P], wo_sb[:],
                              start=True, stop=True)
                inc(last, "attny_ready")

            def x1_transposes(b):
                pe.wait_ge(s["x1_ready"], TB * (b + 1))
                for t in range(TB):
                    last = nc.tensor.transpose(PS[:, 4, t * P:(t + 1) * P], x1[:, t, :], ident)
                inc(last, "x1T_ready")

            def cross_queries(b):
                pe.wait_ge(s["x1T_sb"], b + 1)
                for qd in (1, 2, 3, 0):
                    inc(mm(PS[0:96, 4 + qd, :], w3[:, 0, qd, :, :].rearrange("p r n -> p (r n)"), x1T[:],
                           start=True, stop=True), "xq_ready")

            def score_maxima(b):
                for n in range(NQ * TB):
                    t, qd = divmod(n, NQ)
                    if n < 2:
                        pe.wait_ge(s["ql_ready"], NQ * (b + 1))
                    else:
                        pe.wait_ge(s["mx_ready"], NQ * TB * b + n - 1)
                    for k in range(2):
                        last = mm(PS[:, 4 + 2 * (n % 2) + k, 0:2 * C], QS[0:96, qd, t * P:(t + 1) * P],
                                  KS[0:96, b, qd, 2 * k:2 * k + 2, :].rearrange("p h c -> p (h c)"),
                                  start=True, stop=True)
                    inc(last, "ms_ready")

            def maxima_transposes(b):
                pe.wait_ge(s["nmx_ready"], b + 1)
                for t in range(TB):
                    last = nc.tensor.transpose(PS[:, 4, t * P:(t + 1) * P], nmx[:, t, :], ident)
                inc(last, "nm_ready")

            def scores(b, i):
                qd, st = divmod(i, 5)
                if i < 2:
                    pe.wait_ge(s["qm_ready"], b + 1)
                else:
                    pe.wait_ge(s["p_ready"], 20 * b + i - 1)
                keys = Kr[:, b, qd, :, :].rearrange("p a n -> p (a n)") if st == 0 else KS[:, b, qd, st - 1, 0:P]
                inc(mm(PS[:, 6 + i % 2, :], keys, QS[:, qd, :], start=True, stop=True), "sc_ready")

            def values(b, i):
                qd, st = divmod(i, 5)
                if st == 0 and qd >= 2:
                    pe.wait_ge(s["ox_sb"], NQ * b + qd - 1)
                pe.wait_ge(s["p_ready"], 20 * b + i + 1)
                if st == 0:
                    last = mm(PS[:, 4 + qd % 2, :], Vr[:, b, qd, :, :].rearrange("p a n -> p (a n)"),
                              Pt[:, i % 4, :], start=True, stop=False, skip_group_check=True)
                else:
                    a = st - 1
                    last = mm(PS[32 * a:32 * a + 32, 4 + qd % 2, :], Vm[:, b, 4 * qd + a, :], Pt[:, i % 4, :],
                              start=False, stop=True, tile_position=(0, 32 * a), skip_group_check=True)
                inc(last, "pv_done")

            def cross_scores(b, between=None):
                scores(b, 0)
                scores(b, 1)
                for i in range(20):
                    values(b, i)
                    if i < 18:
                        scores(b, i + 2)
                    if between and i in between:
                        between[i]()

            def head_rows(b):
                for t in range(TB):
                    pe.wait_ge(s["ox_sb"], NQ * (b + 1))
                    for qd in range(NQ):
                        last = nc.tensor.transpose(PS[:, 4 + t, qd * P:(qd + 1) * P],
                                                   Osb[:, qd, t * P:(t + 1) * P], ident)
                    inc(last, "xt_ready")

            def norm_transposes(b):
                pe.wait_ge(s["on_ready"], b + 1)
                for t in range(TB):
                    last = nc.tensor.transpose(
                        PS[:, 4, t * P:(t + 1) * P],
                        On[:, t * H:(t + 1) * H, :].rearrange("p h k -> p (h k)"), ident)
                inc(last, "onT_ready")

            def cross_projection(b):
                pe.wait_ge(s["onT_sb"], b + 1)
                for t in range(TB):
                    last = mm(PS[:, 5, t * P:(t + 1) * P], OnT[:, t * P:(t + 1) * P], xwo, start=True, stop=True)
                inc(last, "xy_ready")

            def x2_transposes(b):
                pe.wait_ge(s["x2_ready"], TB * (b + 1))
                for t in range(TB):
                    last = nc.tensor.transpose(PS[:, 6, t * P:(t + 1) * P], x2[:, b, t, :], ident)
                inc(last, "x2T_ready")

            def logits(b):
                pe.wait_ge(s["rc_ready"], 1)
                pe.wait_ge(s["x2L_ready"], b + 1)
                for t in range(TB):
                    o, blk = PS[:, 7, t * E:(t + 1) * E], slice(t * P, (t + 1) * P)
                    mm(o, x2H[:, b, blk], rcH[:], start=True, stop=False)
                    mm(o, x2H[:, b, blk], rcL[:], start=False, stop=False)
                    last = mm(o, x2L[:, b, blk], rcH[:], start=False, stop=True)
                inc(last, "lg_ready")

            def gate_transposes(b):
                pe.wait_ge(s["g_ready"], b + 1)
                for t in range(TB):
                    last = nc.tensor.transpose(PS[0:E, 4, t * P:(t + 1) * P], gates[:, b * TB + t, :], ident)
                inc(last, "gT_ready")

            def bias_rows(b):
                pe.wait_ge(s["gT_sb"], b + 1)
                for t in range(TB):
                    last = mm(PS[:, 5, t * P:(t + 1) * P], gatesT[:, t * P:(t + 1) * P], b2_sb[:], start=True, stop=True)
                inc(last, "acc_in_ready")

            def setup():
                pe.wait_ge(s["ld_late"], 16 * N_LATE)
                pe.wait_ge(s["w3_ready"], 1)
                pe.wait_ge(s["keysq_ready"], 1)
                inc(mm(PS[:, 4, 0:E], onesq[:], keysq[:], start=True, stop=True), "key_ready")
                pe.wait_ge(s["ctxR_ready"], 1)
                for b in range(B):
                    mm(PS[:, 5, b * D:(b + 1) * D], ctxT_sb[:, b, 0:P], xwv, start=True, stop=True)
                    last = mm(PS[:, 5, (B + b) * D:(B + b + 1) * D], ctxR[:, b, :, :].rearrange("p a n -> p (a n)"),
                              xwv, start=True, stop=True)
                inc(last, "vx_ready")
                for qd in range(NQ):
                    if qd >= 2:
                        pe.wait_ge(s["kx_sb"], qd - 1)
                    inc(mm(PS[0:96, 6 + qd % 2, 0:B * C], w3[:, 1, qd, :, :].rearrange("p r n -> p (r n)"),
                           ctxT_sb[:].rearrange("p b c -> p (b c)"), start=True, stop=True), "kx_ready")
                pe.wait_ge(s["kE_sb"], 1)
                pe.wait_ge(s["kx_sb"], NQ)

            def up(b, u, r=0):
                k = u % 2
                pe.wait_ge(s["ws_ready"], r + (E * b + u + 1))
                for c in range(FC):
                    n = FC * u + c
                    ring = 3 if b == 0 else 4
                    if n >= ring or not isinstance(r, int):
                        pe.wait_ge(s["gelu_ready"], r * FC + (FC * E * b + n - ring + 1))
                    o, blk = PS[:, h_bank(b, n), :], slice(c * P, (c + 1) * P)
                    mm(o, w1H[:, k, blk], x2H[:, b, :], start=True, stop=False)
                    mm(o, w1H[:, k, blk], x2L[:, b, :], start=False, stop=False)
                    inc(mm(o, w1L[:, k, blk], x2H[:, b, :], start=False, stop=True), "h_ready")

            def down(b, u, r=0):
                pe.wait_ge(ld_w2[u % 2], r * 16 + 32 * ((E * b + u) // 2 + 1))
                pe.wait_ge(s["gelu_ready"], r * FC + FC * (E * b + u + 1))
                ring = 1 if b == 0 else 2
                if u >= ring or not isinstance(r, int):
                    pe.wait_ge(s["acc_done"], r * TB + TB * (E * b + u - ring + 1))
                for t in range(TB):
                    for c in range(FC):
                        last = mm(PS[:, y_bank(b, u), t * P:(t + 1) * P], hid[:, u % 2, c, t * P:(t + 1) * P],
                                  w2_sb[:, u % 2, c, :], start=(c == 0), stop=(c == FC - 1))
                inc(last, "y_ready")

            pe.wait_ge(s["ld_first"], 16 * N_FIRST)
            pe.wait_ge(s["wrep_ready"], 1)
            for item in ("k", "q", "zb", "zf"):
                front(0, item)
            pe.wait_ge(s["ld_attn"], 16 * (N_ATTN - N_FIRST))
            pe.wait_ge(s["wrep_ready"], 2)
            for item in ["gh" if x == "ksum" else "ksum" if x == "gh" else x for x in FRONT[4:]]:
                front(0, item)
            setup()
            for item in ["k", "q"] + FRONT[2:11]:
                front(1, item)
            solutions(0)
            head_outputs(0)
            front(1, ("rep", 4))
            head_squares(0)
            front(1, ("rep", 5))
            front(1, ("rep", 6))
            attn_projection(0)
            front(1, ("rep", 7))
            x1_transposes(0)
            front(1, ("rep", 8))
            cross_queries(0)
            front(1, ("rep", 9))
            for m in range(4):
                front(1, ("tr", m))
            pe.wait_ge(s["ks_ready"], 1)
            score_maxima(0)
            maxima_transposes(0)
            pe.wait_ge(s["v_ready"], 1)
            fill = [("rep", DH + 2), ("rep", DH + 3)] + [("tr", m) for m in range(4, 8)] + [
                ("rep", n) for n in range(DH + 4, 2 * DH)]
            cross_scores(0, {1 + 2 * n if n < 9 else 19: (lambda x=x: front(1, x)) for n, x in enumerate(fill)})
            head_rows(0)
            norm_transposes(0)
            cross_projection(0)
            x2_transposes(0)
            logits(0)
            gate_transposes(0)
            bias_rows(0)
            pe.wait_ge(s["rep_used"], 32)
            pe.wait_ge(s["m_ready"], 16)
            up(0, 0)
            tail = {4: [solutions], 5: [head_outputs], 6: [head_squares], 7: [attn_projection], 8: [x1_transposes],
                    9: [cross_queries], 10: [score_maxima, maxima_transposes], 11: [cross_scores], 12: [head_rows],
                    13: [norm_transposes, cross_projection], 14: [x2_transposes, logits],
                    15: [gate_transposes, bias_rows]}
            for u in range(E):
                if u < E - 1:
                    up(0, u + 1)
                down(0, u)
                for part in tail.get(u, ()):
                    part(1)
            pe.wait_ge(s["gelu_ready"], FC * E)
            pe.wait_ge(s["acc_done"], TB * E)
            pe.wait_ge(s["acc_init"], 2)
            up(1, 0)
            with pe.Fori(0, E - 2, 2) as r:
                up(1, 1, r)
                down(1, 0, r)
                up(1, 2, r)
                down(1, 1, r)
            up(1, E - 1)
            down(1, E - 2)
            down(1, E - 1)

        @block.scalar
        def _(act):
            A = nc.scalar.activation
            count = {}

            def step(ins, name="act_chain"):
                ins.then_inc(s[name], 1)
                count[name] = count.get(name, 0) + 1
                act.wait_ge(s[name], count[name])

            def copy(dst, src, name):
                step(nc.scalar.copy(dst, src), name)

            def rsqrt(dst, src, name, scale=1.0, eps=L2_EPS):
                step(A(dst, src, ACT.Ln, bias=epst[:, 0:1] if eps == L2_EPS else epst[:, 1:2], scale=scale))
                step(A(dst, dst, ACT.Exp, scale=-0.5), name)

            def front(b):
                bank = {x: PS[:, front_bank(x), :] for x in FRONT}
                act.wait_ge(s["k_ready"], b + 1)
                step(A(sq, bank["k"], ACT.Square), "ksq_ready")
                if b:
                    act.wait_ge(s["kk_free"], b)
                copy(kbeta, bank["k"], "kcp_ready")
                act.wait_ge(s["q_ready"], b + 1)
                step(A(qsq, bank["q"], ACT.Square), "qsq_ready")
                copy(qtok, bank["q"], "qcp_ready")
                act.wait_ge(s["zb_ready"], b + 1)
                step(A(beta, bank["zb"], ACT.Sigmoid), "beta_ready")
                act.wait_ge(s["zf_ready"], b + 1)
                step(A(fgt[:], bank["zf"], ACT.Sigmoid, bias=delta_col), "f_ready")
                act.wait_ge(s["gh_ready"], b + 1)
                copy(gateh, bank["gh"][0:DH, :], "ghc_ready")
                act.wait_ge(s["g2_ready"], b + 1)
                step(A(gateT[:, b, :], bank["g2"], ACT.Sigmoid), "gate_ready")
                nc.scalar.preload_act_table_set(LNEXP)
                act.wait_ge(s["ksum_ready"], b + 1)
                rsqrt(kinv, bank["ksum"], "kinv_ready")

            def query_norms(b):
                act.wait_ge(s["qss_ready"], b + 1)
                rsqrt(qinv[:], qss[:], "qinv_ready")

            def states(b, ms):
                for m in ms:
                    half, t = divmod(m, TB)
                    act.wait_ge(s["tr_ready"], 2 * TB * b + m + 1)
                    copy(M[:, :, 4 * half:4 * half + 4, t * H:(t + 1) * H].rearrange("p i j h -> p j h i"),
                         PS[:, front_bank(("tr", m)), :].rearrange("p (j h i) -> p j h i", j=4, h=H), "m_ready")

            def head_squares(b):
                act.wait_ge(s["og_ready"], b + 1)
                step(A(osq[:], og[:], ACT.Square), "ogsq_ready")

            def head_norms(b):
                act.wait_ge(s["ogms_ready"], b + 1)
                rsqrt(orr[:], PS[:, 6, :], "ogr_ready", scale=1.0 / DH, eps=NORM_EPS)

            def layer_rstd(n):
                act.wait_ge(s["stats_ready"], n)
                rsqrt(rstd[:], mv[:, :, 1], "rstd_ready", eps=NORM_EPS)

            def x1_columns(b):
                act.wait_ge(s["x1T_ready"], b + 1)
                copy(x1T[:], PS[:, 4, :], "x1T_sb")

            def cross_queries(b):
                for n, qd in enumerate((1, 2, 3, 0)):
                    act.wait_ge(s["xq_ready"], NQ * b + n + 1)
                    step(A(QS[0:96, qd, :], PS[0:96, 4 + qd, :], ACT.Identity, bias=cols_sb[0:96, 3 + qd:4 + qd]),
                         "qh_ready")

            def maxima(b):
                act.wait_ge(s["nm_ready"], b + 1)
                act.wait_ge(s["v_ready"], B)
                copy(mh[96:P, :], PS[96:P, 4, :], "mh_ready")

            def exps(b, i):
                act.wait_ge(s["sc_ready"], 20 * b + i + 1)
                if i >= 4:
                    act.wait_ge(s["pv_done"], 20 * b + i - 3)
                step(A(Pt[:, i % 4, :], PS[:, 6 + i % 2, :], ACT.Exp, scale=SM_SCALE), "p_ready")

            def norm_columns(b):
                act.wait_ge(s["onT_ready"], b + 1)
                copy(OnT[:], PS[:, 4, :], "onT_sb")

            def token_squares(b):
                act.wait_ge(s["x2_ready"], TB * (b + 1))
                for t in range(TB):
                    step(A(osq[:, t * P:(t + 1) * P], x2[:, b, t, :], ACT.Square, accum_out=xsq[:, t:t + 1]),
                         "xsq_ready")

            def x2_columns(b):
                act.wait_ge(s["x2T_ready"], b + 1)
                copy(x2H[:, b, :], PS[:, 6, :], "x2H_ready")

            def top_weights(b):
                act.wait_ge(s["w4_diff"], b + 1)
                step(A(w4[:], w4[:], ACT.Exp), "w4_ready")

            def gate_columns(b):
                act.wait_ge(s["gT_ready"], b + 1)
                copy(gatesT, PS[0:E, 4, :], "gT_sb")

            def gelu(b, u, r=0):
                for c in range(FC):
                    n = FC * u + c
                    act.wait_ge(s["h_ready"], r * FC + (FC * E * b + n + 1))
                    if c == 0:
                        act.wait_ge(ld_w2[u % 2], r * 16 + 32 * ((E * b + u) // 2 + 1))
                        if E * b + u >= 2:
                            act.wait_ge(s["y_ready"], r + (E * b + u - 1))
                    A(hid[:, u % 2, c, :], PS[:, h_bank(b, n), :], ACT.Gelu, bias=b1_sb[:, u % 2, c:c + 1]).then_inc(
                        s["gelu_ready"], 1)

            act.wait_ge(s["pool_set"], 1)
            act.wait_ge(s["ld_first"], 16 * N_FIRST)
            front(0)
            act.wait_ge(s["ld_attn"], 16 * (N_ATTN - N_FIRST))
            step(A(softtmp, lamb_row, ACT.Abs))
            step(A(softtmp, softtmp, ACT.Exp, scale=-1.0))
            step(A(softtmp, softtmp, ACT.Ln, bias=1.0), "lamb_ln")
            query_norms(0)
            act.wait_ge(s["ld_late"], 16 * N_LATE)
            step(A(keysq[:], keysrw_sb[:, 0, :], ACT.Square), "keysq_ready")
            states(0, range(8))
            act.wait_ge(s["key_ready"], 1)
            copy(kE, PS[:, 4, 0:E], "kE_sb")
            act.wait_ge(s["vx_ready"], 1)
            copy(vx.rearrange("p k b n -> p (k b n)"), PS[:, 5, :], "vx_sb")
            for qd in range(NQ):
                act.wait_ge(s["kx_ready"], qd + 1)
                step(A(kx[0:96, qd, :], PS[0:96, 6 + qd % 2, 0:B * C], ACT.Identity,
                       bias=cols_sb[0:96, 3 + NQ + qd:4 + NQ + qd]), "kx_sb")
            front(1)
            query_norms(1)
            head_squares(0)
            head_norms(0)
            layer_rstd(1)
            x1_columns(0)
            cross_queries(0)
            states(1, range(4))
            maxima(0)
            for i in range(20):
                exps(0, i)
                if i in (8, 10, 12, 14):
                    states(1, [4 + (i - 8) // 2])
            norm_columns(0)
            layer_rstd(2)
            x2_columns(0)
            token_squares(0)
            top_weights(0)
            gate_columns(0)
            tail = {5: [head_squares], 6: [head_norms], 7: [lambda b: layer_rstd(3)], 8: [x1_columns],
                    9: [cross_queries], 10: [maxima], 11: [lambda b: [exps(b, i) for i in range(20)]],
                    13: [norm_columns, lambda b: layer_rstd(4)], 14: [x2_columns, token_squares, top_weights],
                    15: [gate_columns]}
            gelu(0, 0)
            for u in range(E):
                if u < E - 1:
                    gelu(0, u + 1)
                for part in tail.get(u, ()):
                    part(1)
            layer_rstd(5)
            gelu(1, 0)
            with act.Fori(0, E - 2, 2) as r:
                gelu(1, 1, r)
                gelu(1, 2, r)
            gelu(1, E - 1)
            layer_rstd(6)

        @block.gpsimd
        def _(pool):
            Gp = nc.gpsimd
            count = {}

            def step(ins, name="pool_chain"):
                ins.then_inc(s[name], 1)
                count[name] = count.get(name, 0) + 1
                pool.wait_ge(s[name], count[name])

            Gp.memset(epst[:, 0:1], L2_EPS)
            step(Gp.memset(epst[:, 1:2], NORM_EPS), "pool_set")
            pool.wait_ge(s["ld_first"], 16 * N_FIRST)
            step(Gp.tensor_copy(wrep[:, 1, :, :].rearrange("p j (h i) -> p j h i", h=H),
                                bc(wqkv_sb[:, 2, :].rearrange("p (h j) -> p j h", h=H), 3, DH)), "wrepv_ready")
            Gp.memset(onesq[:], 1.0)
            Gp.memset(f(Kr[:]), 0.0)
            Gp.memset(Vr[:], 0.0)
            Gp.memset(nmx[:], 0.0)
            Gp.memset(Vm[:], 0.0)
            step(Gp.memset(ctxR, 0.0))
            pool.wait_ge(s["ld_attn"], 16 * (N_ATTN - N_FIRST))
            step(Gp.tensor_copy(ctxR[:, :, :, 0:CR], bc(ctxT_sb[:, :, P:C], 2, 4)), "ctxR_ready")
            pool.wait_ge(s["lamb_ln"], 1)
            step(Gp.tensor_scalar(lamb[:], lamb_row, 0.0, LAMBDA_LOWER, ALU.max, ALU.add))
            step(Gp.tensor_tensor(lamb[:], lamb[:], softtmp, ALU.add), "lamb_ready")
            pool.wait_ge(s["ld_late"], 16 * N_LATE)
            for k in range(2):
                last = Gp.tensor_copy(w3[:, k], bc(xw_sb[:, k, :].rearrange("p (q n) -> p q n", q=NQ), 2, 3))
                if k == 0:
                    step(last)
            step(last, "w3_ready")
            step(Gp.tensor_scalar(rcomb[:], keysrw_sb[:, 0, :], 2.0, None, ALU.mult))
            step(Gp.tensor_tensor(rcomb[:], rcomb[:], keysrw_sb[:, 1, :], ALU.add))
            step(Gp.tensor_copy(rcH[:], rcomb[:]))
            step(Gp.tensor_tensor(rcL[:], rcomb[:], f(rcH[:]), ALU.subtract), "rc_ready")
            pool.wait_ge(s["kE_sb"], 1)
            step(Gp.tensor_tensor(cE[:], rb_row, kE, ALU.subtract), "cE_ready")
            pool.wait_ge(s["kx_sb"], NQ)
            step(Gp.tensor_copy(kxS, kx[0:96]))
            step(Gp.tensor_tensor(kxS[32:64], kx[32:64], f(kxS[32:64]), ALU.subtract))
            for b in range(B):
                for qd in range(NQ):
                    step(Gp.tensor_tensor(KS[0:96, b, qd, :, :], bc(f(kxS[:, qd, b * C:(b + 1) * C]), 1, 4),
                                          bc(hmask[0:96, qd, :], 2, C), ALU.mult))
                    step(Gp.tensor_copy(KS[96:P, b, qd, :, :], bc(hmask[96:P, qd, :], 2, C)))
                step(Gp.tensor_copy(Kr[:, b, :, :, 0:CR].rearrange("p q a n -> p (q a) n"),
                                    f(KS[:, b, :, :, P:C]).rearrange("p q a n -> p (q a) n")), "ks_ready")
            pool.wait_ge(s["vx_sb"], 1)
            for b in range(B):
                step(Gp.tensor_tensor(Vm[:, b, :, 0:DH], vx[:, 0, b, :].rearrange("p (h k) -> p h k", h=H),
                                      bv_row.rearrange("p (h k) -> p h k", h=H), ALU.add))
                step(Gp.memset(Vm[:, b, :, DH:DH + 1], 1.0))
                for a in range(4):
                    rows = slice(32 * a, 32 * a + CR)
                    step(Gp.tensor_tensor(
                        Vr[rows, b, :, a, 0:DH],
                        vx[rows, 1, b, :].rearrange("p (q a k) -> p q a k", q=NQ, a=4)[:, :, a, :],
                        bv_row[rows, :].rearrange("p (q a k) -> p q a k", q=NQ, a=4)[:, :, a, :], ALU.add))
                    last = Gp.memset(Vr[rows, b, :, a, DH:DH + 1], 1.0)
                    if a < 3:
                        step(last)
                step(last, "v_ready")
            def split(k, n):
                def chunks(w):
                    return w[:, k, :].rearrange("p (c n) -> p c n", c=FC)

                pool.wait_ge(ld_w1[k], n * 16 + 16)
                Gp.tensor_tensor(chunks(w1H), chunks(w1_sb), bc(onesq[:], 1, FC), ALU.mult).then_inc(wh_ready[k], 1)
                pool.wait_ge(wh_ready[k], n + 1)
                Gp.tensor_tensor(w1L[:, k, :], w1_sb[:, k, :], f(w1H[:, k, :]), ALU.subtract).then_inc(
                    s["ws_ready"], 1)

            for k in range(2):
                split(k, 0)
            with pool.Fori(1, B * E // 2) as n:
                for k in range(2):
                    pool.wait_ge(s["h_ready"], n * (2 * FC) + (FC * (k - 1)))
                    split(k, n)

        @block.vector
        def _(dve):
            V = nc.vector
            count = {}

            def step(ins, name="dve_chain"):
                ins.then_inc(s[name], 1)
                count[name] = count.get(name, 0) + 1
                dve.wait_ge(s[name], count[name])

            def tt(o, a, c, op, name="dve_chain"):
                step(V.tensor_tensor(o, a, c, op), name)

            def flat(ap):
                return ap.rearrange("p t d -> p (t d)")

            def layer_stats(src=res):
                for t in range(TB):
                    step(V.bn_stats(stats[:, t, :], src[:, t, :]))
                for t in range(TB):
                    last = V.bn_aggr(mv[:, t, :], stats[:, t, :])
                    if t < TB - 1:
                        step(last)
                step(last, "stats_ready")

            def normalise(dst, signal, src=res):
                dve.wait_ge(s["rstd_ready"], count["stats_ready"])
                for t in range(TB):
                    step(V.tensor_scalar(dst[:, t, :], src[:, t, :], mv[:, t, 0:1], rstd[:, t:t + 1],
                                         ALU.subtract, ALU.mult), signal)

            def key_vectors(b):
                dve.wait_ge(s["qsq_ready"], b + 1)
                step(V.tensor_reduce(qss[:], qsq.rearrange("p (g i) -> p g i", i=DH), AX.X, ALU.add), "qss_ready")
                dve.wait_ge(s["kcp_ready"], b + 1)
                dve.wait_ge(s["beta_ready"], b + 1)
                tt(kbeta, kbeta, beta, ALU.mult)
                dve.wait_ge(s["kinv_ready"], b + 1)
                tt(kbeta, kbeta, kinv, ALU.mult)
                tt(kc[:], kbeta, kinv, ALU.mult, "kvec_ready")
                dve.wait_ge(s["f_ready"], b + 1)

            def scan(b, n):
                j = n % DH
                dve.wait_ge(s["rep_ready"], 16 * b + n + 1)
                tt(prod, (kc if n < DH else kbeta)[:], PS[:, front_bank(("rep", n)), :], ALU.mult, "rep_used")
                name = "kk_ready" if n < DH else "kk_free" if n == 2 * DH - 1 else "dve_chain"
                step(V.tensor_tensor_scan((Akk if n < DH else Akv)[:, j, :], fgt[:], prod, 0.0,
                                          ALU.mult, ALU.add), name)

            def right_sides(b):
                dve.wait_ge(s["qinv_ready"], b + 1)
                dve.wait_ge(s["qcp_ready"], b + 1)
                tt(M[:, :, DH, :].rearrange("p i g -> p g i"), qtok.rearrange("p (g i) -> p g i", i=DH),
                   bc(qinv[:], 2, DH), ALU.mult, "qn_ready")

            def diagonal(b):
                dve.wait_ge(s["m_ready"], 8 * (b + 1))
                dve.wait_ge(s["lamb_ready"], 1)
                Md = M[:].rearrange("p i j g -> p (i j) g")[:, 0:DH * (DH + 1):DH + 2, :].rearrange(
                    "p i (t h) -> p i t h", t=TB)
                tt(Md, Md, bc(lamb[:].rearrange("p (h i) -> p i h", h=H), 2, TB), ALU.add)

            def eliminate(b, k):
                n = DH - 1 - k
                step(V.reciprocal(rpiv[:], M[:, k, k, :]))
                tt(U[:, k, k:, :], M[:, k, k + 1:, :], bc(rpiv[:], 1, n + 1), ALU.mult)
                cut = k + 1 + (n // 2 if n >= 4 else n)
                for i0, i1 in ((k + 1, cut), (cut, DH)):
                    ni, nj = i1 - i0, DH + 1 - i0
                    if ni > 0:
                        upd = tmp[:, 0:ni * nj * G].rearrange("p (i j g) -> p i j g", i=ni, j=nj)
                        tt(upd, bc(M[:, k, i0:i1, :], 2, nj), bc(U[:, k, i0 - 1:, :], 1, ni), ALU.mult)
                        tt(M[:, i0:i1, i0:, :], M[:, i0:i1, i0:, :], upd, ALU.subtract)

            def substitute(b):
                y = U[:, :, DH - 1, :]
                for j in range(DH - 1, 0, -1):
                    upd = tmp[:, 0:j * G].rearrange("p (i g) -> p i g", i=j)
                    tt(upd, U[:, 0:j, j - 1, :], bc(y[:, j, :], 1, j), ALU.mult)
                    tt(y[:, 0:j, :], y[:, 0:j, :], upd, ALU.subtract)
                step(V.tensor_copy(xsol[:].rearrange("p (g i) -> p i g", i=DH), y), "solved")

            def outputs(b):
                dve.wait_ge(s["qsT_ready"], b + 1)
                for j in range(DH):
                    tt(Akv[:, j, :], Akv[:, j, :], PS[:, 4, :], ALU.mult, "okv_ready")

            def gated(b):
                dve.wait_ge(s["oT_ready"], b + 1)
                dve.wait_ge(s["gate_ready"], b + 1)
                tt(og[:], PS[:, 5, :], gateT[:, b, :], ALU.mult, "og_ready")

            def head_normed(b):
                dve.wait_ge(s["ogr_ready"], b + 1)
                step(V.scalar_tensor_tensor(attn[:], og[:], normw_col, orr[:], ALU.mult, ALU.mult), "attn_ready")

            def attn_residual(b):
                dve.wait_ge(s["attny_ready"], b + 1)
                tt(flat(res[:]), flat(x_sb[:, b]), PS[:, 7, :], ALU.add)
                layer_stats()

            def x1_rows(b):
                normalise(x1, "x1_ready")
                tt(x1b, x1, bc(bo_row, 1, TB), ALU.add)

            def cross_queries(b):
                for n, qd in enumerate((1, 2, 3, 0)):
                    dve.wait_ge(s["qh_ready"], NQ * b + n + 1)
                    step(V.scalar_tensor_tensor(QS[64:96, qd, :], PS[64:96, 4 + qd, :], cols_sb[64:96, 3 + qd:4 + qd],
                                                f(QS[64:96, qd, :]), ALU.add, ALU.subtract), "ql_ready")

            def score_maxima(b):
                for n in range(NQ * TB):
                    t, qd = divmod(n, NQ)
                    dve.wait_ge(s["ms_ready"], NQ * TB * b + n + 1)
                    k = 4 + 2 * (n % 2)
                    step(V.tensor_reduce(nmx[:, t, 96 + 8 * qd:100 + 8 * qd].rearrange("p (k h) -> p k h", k=2),
                                         PS[:, k:k + 2, 0:2 * C].rearrange("p k (h c) -> p k h c", h=2),
                                         AX.X, ALU.max, negate=True), "mx_ready")
                m = nmx[:, :, 96:].rearrange("p t (q n) -> p t q n", n=8)
                step(V.tensor_copy(m[:, :, :, 4:8], m[:, :, :, 0:4]), "nmx_ready")

            def maxima(b):
                dve.wait_ge(s["mh_ready"], b + 1)
                step(V.scalar_tensor_tensor(mh[96:P, :], f(mh[96:P, :]), lowneg_col[96:P], PS[96:P, 4, :],
                                            ALU.mult, ALU.add))
                step(V.tensor_copy(QS[96:P, :, :], bc(f(mh[96:P, :]), 1, NQ)), "qm_ready")

            def head_sums(b, qd):
                dve.wait_ge(s["pv_done"], 20 * b + 5 * (qd + 1))
                step(V.tensor_copy(Osb[:, qd, :], PS[:, 4 + qd % 2, :]), "ox_sb")

            def head_rows(b):
                dve.wait_ge(s["xt_ready"], TB * (b + 1))
                T = PS[:, 4:8, :].rearrange("p t (h w) -> p (t h) w", w=32)
                step(V.reciprocal(rden[:], T[:, :, DH]))
                tt(On, T[:, :, 0:DH], bc(rden[:], 2, DH), ALU.mult, "on_ready")

            def cross_residual(b):
                dve.wait_ge(s["xy_ready"], b + 1)
                tt(flat(res[:]), flat(x1b), PS[:, 5, :], ALU.add)
                layer_stats()

            def x2_rows(b):
                normalise(x2[:, b], "x2_ready")

            def x2_low(b):
                dve.wait_ge(s["x2H_ready"], b + 1)
                tt(x2L[:, b, :], PS[:, 6, :], f(x2H[:, b, :]), ALU.subtract, "x2L_ready")

            def choose(b):
                dve.wait_ge(s["lg_ready"], b + 1)
                dve.wait_ge(s["cE_ready"], 1)
                tt(logit[:], PS[:, 7, 0:TB * E].rearrange("p (t e) -> p t e", t=TB), bc(cE[:], 1, TB), ALU.add)
                dve.wait_ge(s["xsq_ready"], TB * (b + 1))
                tt(logit[:], logit[:], bc(xsq[:], 2, E), ALU.subtract)
                for t in range(TB):
                    step(V.max(top8[:, t, :], logit[:, t, :]))
                tt(w4[:], top8[:, :, 0:TOPK], bc(top8[:, :, 0], 2, TOPK), ALU.subtract, "w4_diff")
                for t in range(TB):
                    step(V.max_index(idx8[:, t, :], top8[:, t, :], logit[:, t, :]))
                step(V.tensor_copy(idx4[:], idx8[:, :, 0:TOPK]))
                tt(oneh[:], bc(iota, 1, TB * TOPK), bc(idx4[:].rearrange("p t r -> p (t r)"), 2, E), ALU.is_equal)

            def weigh(b):
                dve.wait_ge(s["w4_ready"], b + 1)
                step(V.tensor_reduce(wsum[:], w4[:], AX.X, ALU.add))
                step(V.reciprocal(wsum[:], wsum[:]))
                tt(w4[:], w4[:], bc(wsum[:], 2, TOPK), ALU.mult)
                tt(oneh[:], oneh[:], bc(w4[:].rearrange("p t r -> p (t r)"), 2, E), ALU.mult)
                step(V.tensor_reduce(gates[:, b * TB:(b + 1) * TB, :],
                                     oneh[:].rearrange("p (t r) e -> p t e r", t=TB), AX.X, ALU.add), "g_ready")

            def start_sums(b):
                dve.wait_ge(s["acc_in_ready"], b + 1)
                tt(flat(acc[:, b]), flat(x2[:, b]), PS[:, 5, :], ALU.add, "acc_init")

            def accumulate(b, u, gate, r=0):
                dve.wait_ge(s["y_ready"], r + (E * b + u + 1))
                for t in range(TB):
                    V.scalar_tensor_tensor(acc[:, b, t, :], PS[:, y_bank(b, u), t * P:(t + 1) * P],
                                           gate[:, t:t + 1], acc[:, b, t, :], ALU.mult, ALU.add).then_inc(
                                               s["acc_done"], 1)

            dve.wait_ge(s["ld_first"], 16 * N_FIRST)
            step(V.tensor_copy(wfb[:].rearrange("p k (h i) -> p (k h) i", h=H), bc(wsmall_sb[:, 0:2 * H], 2, DH)),
                 "wrep_ready")
            step(V.tensor_copy(wrep[:, 0, :, :].rearrange("p j (h i) -> p j h i", h=H),
                               bc(wqkv_sb[:, 1, :].rearrange("p (h j) -> p j h", h=H), 3, DH)), "wrep_ready")
            key_vectors(0)
            for n in range(DH):
                scan(0, n)
            right_sides(0)
            for n in range(DH, 2 * DH):
                scan(0, n)
            diagonal(0)
            for k in range(DH):
                eliminate(0, k)
            substitute(0)
            key_vectors(1)
            outputs(0)
            scan(1, 0)
            gated(0)
            scan(1, 1)
            scan(1, 2)
            head_normed(0)
            scan(1, 3)
            attn_residual(0)
            scan(1, 4)
            x1_rows(0)
            scan(1, 5)
            scan(1, 6)
            scan(1, 7)
            scan(1, 8)
            scan(1, 9)
            cross_queries(0)
            score_maxima(0)
            maxima(0)
            right_sides(1)
            for qd, before in enumerate(((10, 11), (), (12,), (13, 14))):
                for n in before:
                    scan(1, n)
                head_sums(0, qd)
            scan(1, 15)
            head_rows(0)
            cross_residual(0)
            x2_rows(0)
            x2_low(0)
            choose(0)
            weigh(0)
            start_sums(0)
            tail = {0: [diagonal, lambda b: eliminate(b, 0), lambda b: eliminate(b, 1)],
                    1: [lambda b, k=k: eliminate(b, k) for k in (2, 3)],
                    2: [lambda b, k=k: eliminate(b, k) for k in (4, 5, 6, 7)], 3: [substitute],
                    4: [outputs], 5: [gated], 6: [head_normed], 7: [attn_residual, x1_rows],
                    9: [cross_queries], 10: [score_maxima, maxima],
                    11: [lambda b, q=q: head_sums(b, q) for q in range(NQ)], 12: [head_rows],
                    13: [cross_residual, x2_rows], 14: [x2_low, choose, weigh],
                    15: [start_sums]}
            for u in range(E):
                accumulate(0, u, gates[:, 0:TB, u])
                for part in tail.get(u, ()):
                    part(1)

            def loop_unit(u, i):
                r = i * 2
                src = gates[:, TB:, :].rearrange("p t (n u) -> p t n u", u=2)[:, :, bass.ds(i, 1), u]
                V.tensor_copy(gslot[:, u, :], src.rearrange("p t o -> p (t o)")).then_inc(s["gslot_ready"], 1)
                dve.wait_ge(s["gslot_ready"], r + (u + 1))
                accumulate(1, u, gslot[:, u, :], r)
                dve.wait_ge(s["acc_done"], r * TB + TB * (E + u + 1))

            def output(b):
                layer_stats(acc[:, b])
                normalise(fin[:, b], "fin_ready", acc[:, b])

            output(0)
            with dve.Fori(0, E // 2) as i:
                loop_unit(0, i)
                loop_unit(1, i)
            output(1)


_OUTS = [((B, S, D), "float32")]


def kernel(**inputs):
    import numpy as np
    import concourse.bacc as bacc
    from concourse.bass_utils import run_bass_kernel_spmd

    a = {k: np.asarray(v) for k, v in inputs.items()}

    def w(name):
        return a["L0_" + name]

    def token_blocks(v):
        return v.reshape(B, TB, P, D).transpose(2, 0, 1, 3)

    r = np.arange(P)
    cols = np.zeros((P, 3 + 2 * NQ), np.float32)
    cols[:, 0] = np.repeat(w("attn_delta"), DH)
    cols[:, 1] = w("attn_norm_weight")
    cols[96:, 2] = -(r[96:] % 8 // 4)
    cols[0:96, 3:3 + NQ] = np.tile(w("xattn_bq").reshape(NQ, 32).T, (3, 1))
    cols[0:96, 3 + NQ:] = np.tile(w("xattn_bk").reshape(NQ, 32).T, (3, 1))
    consts = np.zeros((P, 2 * P + DH * P + NQ * 4 + E), np.float32)
    consts[:, 0:P] = np.eye(P)
    consts[:, P:2 * P] = r[:, None] // DH == r[None, :] // DH
    for j in range(DH):
        consts[:, 2 * P + j * P:2 * P + (j + 1) * P] = (r[:, None] // DH == r[None, :] // DH) & (r[None, :] % DH == j)
    hm = consts[:, 2 * P + DH * P:2 * P + DH * P + NQ * 4].reshape(P, NQ, 4)
    hm[0:96] = (r[0:96] % 32 // DH)[:, None, None] == np.arange(4)
    hm[96:] = ((r[96:] - 96) // 8)[:, None, None] == np.arange(NQ)[:, None]
    hm[96:] *= (r[96:] % 4)[:, None, None] == np.arange(4)
    consts[:, 2 * P + DH * P + NQ * 4:] = np.arange(E)
    consts[:, 2 * P + DH * P:2 * P + DH * P + NQ * 4] = hm.reshape(P, NQ * 4)
    arrays = {
        "xTok": token_blocks(a["x"]),
        "xT": a["x"].transpose(2, 0, 1),
        "ctxT": a["ctx_1024"].transpose(2, 0, 1),
        "wqkv": np.stack([w("attn_Wq"), w("attn_Wk"), w("attn_Wv")], 1),
        "wsmall": np.concatenate([w("attn_Wf"), w("attn_Wbet"), w("attn_gate_w1")], 1),
        "gw2": w("attn_gate_w2"),
        "wo": w("attn_Wo"),
        "cols": cols,
        "lamb": w("attn_lamb_params"), "bv": w("xattn_bv"), "bo": w("xattn_bo"), "rb": w("ffn_rb"),
        "xw": np.stack([w("xattn_Wq"), w("xattn_Wk"), w("xattn_Wv"), w("xattn_Wo")], 1),
        "keysrw": np.stack([w("ffn_keys").T, w("ffn_rw").T], 1),
        "b2": w("ffn_b2"),
        "w1T": w("ffn_w1").transpose(0, 2, 1),
        "w2T": w("ffn_w2").transpose(0, 2, 1).reshape(E, FC, P, D).transpose(0, 2, 1, 3),
        "b1T": w("ffn_b1").reshape(E, FC, P).transpose(0, 2, 1),
        "consts": consts,
    }
    arrays = {k: np.ascontiguousarray(v) for k, v in arrays.items()}
    nc = bacc.Bacc("TRN2", target_bir_lowering=False, num_devices=1)
    t = {k: nc.dram_tensor(f"in_{k}", v.shape, F32, kind="ExternalInput").ap() for k, v in arrays.items()}
    out = nc.dram_tensor("out", (B, S, D), F32, kind="ExternalOutput").ap()
    rows = [t.pop(k).rearrange("(o n) -> o n", o=1).broadcast_to((P, n))
            for k, n in (("lamb", D), ("bv", D), ("bo", D), ("rb", E))]
    decoder_layer(nc, rowsb=rows, out=out.rearrange("b (t p) d -> p b t d", p=P), **t)
    r = run_bass_kernel_spmd(nc, [{f"in_{k}": v for k, v in arrays.items()}], core_ids=[0])
    return r.results[0]["out"]
```

```python
from contextlib import ExitStack

import concourse.bass as bass
from concourse import mybir

F32 = mybir.dt.float32
F32R = mybir.dt.float32r
U32 = mybir.dt.uint32
ALU = mybir.AluOpType
ACT = mybir.ActivationFunctionType
AX = mybir.AxisListType

P = 128
B, S, D = 2, 512, 128
H, DH = 16, 8
TB = S // P
G = TB * H
C = 154
CR = C - P
NQ = H // 4
E, F = 16, 512
FC = F // P
TOPK = 4
LAMBDA_LOWER = 0.25
L2_EPS = 1e-6
NORM_EPS = 1e-5
SM_SCALE = DH ** -0.5
LNEXP = "natural_log_exp_and_others"
GELU_SET = "gelu_and_others"


def bc(ap, axis, n):
    v = ap.unsqueeze(axis)
    shape = list(v.shape)
    shape[axis] = n
    return v.broadcast_to(tuple(shape))


def decoder_layer(nc, xTok, xT, ctxT, wqkv, wsmall, gw2, wo, cols, rowsb, xw, keysrw, b2, w1T, w2T, b1T, consts, out):
    ctx = ExitStack()
    with ctx:
        def sb(name, shape, dt=F32):
            return ctx.enter_context(nc.sbuf_tensor(name, shape, dt))

        def sem(name):
            return ctx.enter_context(nc.semaphore(name))

        def f(ap):
            return ap.bitcast(F32)

        PS = ctx.enter_context(nc.psum_tensor("PS", [P, 8, 512], F32))

        epst = sb("epst", [P, 2])
        x_sb = sb("x_sb", [P, B, TB, D])
        xT_sb = sb("xT_sb", [P, B, S])
        ctxT_sb = sb("ctxT_sb", [P, B, C])
        wqkv_sb = sb("wqkv_sb", [P, 3, D])
        wsmall_sb = sb("wsmall_sb", [P, 2 * H + DH])
        gw2_sb = sb("gw2_sb", [DH, D])
        wo_sb = sb("wo_sb", [P, D])
        cols_sb = sb("cols_sb", [P, 3 + 2 * NQ])
        rows_sb = sb("rows_sb", [P, 3 * D + E])
        xw_sb = sb("xw_sb", [P, 4, D])
        keysrw_sb = sb("keysrw_sb", [P, 2, E])
        b2_sb = sb("b2_sb", [E, D])
        const_sb = sb("const_sb", [P, 2 * P + DH * P + NQ * 4 + E])
        delta_col, normw_col, lowneg_col = (cols_sb[:, i:i + 1] for i in range(3))
        lamb_row, bv_row, bo_row = (rows_sb[:, i * D:(i + 1) * D] for i in range(3))
        rb_row = rows_sb[:, 3 * D:3 * D + E]
        ident = const_sb[:, 0:P]
        headones = const_sb[:, P:2 * P]
        sel = const_sb[:, 2 * P:2 * P + DH * P].rearrange("p (j n) -> p j n", j=DH)
        hmask = const_sb[:, 2 * P + DH * P:2 * P + DH * P + NQ * 4].rearrange("p (q a) -> p q a", q=NQ)
        iota = const_sb[:, 2 * P + DH * P + NQ * 4:]
        wq = wqkv_sb[:, 0, :]
        gw1 = wsmall_sb[:, 2 * H:2 * H + DH]
        xwq, xwk, xwv, xwo = (xw_sb[:, i, :] for i in range(4))

        wrep = sb("wrep", [P, 2, DH, D])
        wfb = sb("wfb", [P, 2, D])
        lamb = sb("lamb", [P, D])
        onesq = sb("onesq", [P, P])
        rcomb = sb("rcomb", [P, E])
        rcH = sb("rcH", [P, E], F32R)
        rcL = sb("rcL", [P, E], F32R)
        keysq = sb("keysq", [P, E])
        cE = sb("cE", [P, E])
        w3 = sb("w3", [P, 2, NQ, 3, 32])
        KS = sb("KS", [P, B, NQ, 4, C], F32R)
        Kr = sb("Kr", [P, B, NQ, 4, 32], F32R)
        Vm = sb("Vm", [P, B, H, 32])
        Vr = sb("Vr", [P, B, NQ, 4, 32])
        nmx = sb("nmx", [P, TB, P])

        hid = sb("hid", [P, 2, FC, S])
        sq, qsq, beta, kinv, qtok, kbeta, prod, gateh = (hid[:, i // FC, i % FC, :] for i in range(2 * FC))
        gateh = gateh[0:DH, :]
        fgt = sb("fgt", [P, S])
        gateT = sb("gateT", [P, B, S])
        kc = sb("kc", [P, S])
        qss = sb("qss", [P, G])
        qinv = sb("qinv", [P, G])
        Akk = sb("Akk", [P, DH, S])
        Akv = sb("Akv", [P, DH, S])
        M = sb("M", [P, DH, DH + 1, G])
        U = Akk[:].rearrange("p k (j g) -> p k j g", g=G)
        tmp = sb("tmp", [P, 24 * G])
        zeros = tmp[:, 0:512]
        rpiv = sb("rpiv", [P, G])
        xsol = sb("xsol", [P, S])
        og = sb("og", [P, S])
        osq = sb("osq", [P, S])
        orr = sb("orr", [P, S])
        attn = osq

        res = sb("res", [P, TB, D])
        stats = sb("stats", [P, TB, 6])
        mv = sb("mv", [P, TB, 2])
        rstd = sb("rstd", [P, TB])
        x1b = res[:]
        x1 = og[:].rearrange("p (t d) -> p t d", t=TB)
        x1T = xsol
        QS = sb("QS", [P, NQ, S], F32R)
        Pt = sb("Pt", [P, 4, S])
        mh = Pt[:, 0, :].bitcast(F32R)
        Osb = sb("Osb", [P, NQ, S])
        rden = sb("rden", [P, TB * H])
        On = osq[:].rearrange("p (t k) -> p t k", k=DH)
        OnT = orr

        x2 = sb("x2", [P, B, TB, D])
        acc = x2
        x2H = sb("x2H", [P, B, S], F32R)
        x2L = sb("x2L", [P, B, S], F32R)
        xsq = sb("xsq", [P, TB])
        logit = sb("logit", [P, TB, E])
        top8 = sb("top8", [P, TB, 8])
        idx8 = sb("idx8", [P, TB, 8], U32)
        idx4 = sb("idx4", [P, TB, TOPK])
        w4 = sb("w4", [P, TB, TOPK])
        wsum = sb("wsum", [P, TB])
        oneh = sb("oneh", [P, TB * TOPK, E])
        gates = sb("gates", [P, B * TB, E])
        gatesT = xsol[0:E, :]
        gslot = sb("gslot", [P, 2, TB])
        w1H = sb("w1H", [P, 2, F], F32R)
        w1L = sb("w1L", [P, 2, F], F32R)
        w1_sb = wrep[:, 0, :, :].rearrange("p j n -> p (j n)").rearrange("p (k n) -> p k n", k=2)
        w2_sb = wrep[:, 1, :, :].rearrange("p j n -> p (j n)").rearrange("p (k c n) -> p k c n", k=2, c=FC)
        b1_sb = sb("b1_sb", [P, 2, FC])
        fin = x_sb
        scratch = Pt[:].rearrange("p r s -> p (r s)")
        kx = scratch[:, 0:NQ * B * C].rearrange("p (q n) -> p q n", q=NQ)
        vx = scratch[:, NQ * B * C:NQ * B * C + 2 * B * D].rearrange("p (k b n) -> p k b n", k=2, b=B)
        kE = scratch[:, 4 * S - E:]
        scratch = Osb[:].rearrange("p q s -> p (q s)")
        kxS = scratch[:, 0:NQ * B * C].bitcast(F32R).rearrange("p (q n) -> p q n", q=NQ)
        ctxR = scratch[:, NQ * B * C:NQ * B * C + B * 4 * 32].rearrange("p (b a n) -> p b a n", b=B, a=4)
        softtmp = scratch[:, 4 * S - D:]

        names = """ld_x ld_first ld_attn ld_late kv_ready pool_set wrepv_ready w3_ready ctxR_ready lamb_ln lamb_ready
        wrep_ready k_ready q_ready zb_ready zf_ready gh_ready g2_ready ksum_ready ksq_ready kcp_ready ghc_ready beta_ready
        f_ready gate_ready qsq_ready qcp_ready kinv_ready qinv_ready kvec_ready qss_ready qn_ready
        rep_ready rep_used eliminated zeros_ready kk_ready tr_ready m_ready solved qsT_ready okv_ready oT_ready og_ready
        ogsq_ready ogms_ready ogr_ready attn_ready attny_ready stats_ready rstd_ready x1_ready x1T_ready x1T_sb
        xq_ready qh_ready ql_ready ms_ready mx_ready nmx_ready nm_ready mh_ready qm_ready sc_ready p_ready pv_done
        ox_sb xt_ready on_ready onT_ready onT_sb xy_ready x2_ready x2T_ready x2H_ready x2L_ready lg_ready xsq_ready
        w4_diff w4_ready g_ready gT_ready gT_sb acc_in_ready acc_init keysq_ready key_ready kE_sb kx_ready kx_sb
        vx_ready vx_sb rc_ready ks_ready v_ready cE_ready kxS_ready pool_rows factor_row ws_ready gslot_ready
        dve_chain act_chain pool_chain h_ready gelu_ready y_ready last_y_ready acc_done out_done fin_ready"""
        s = {n: sem(n) for n in names.split()}
        ld_w1 = [sem(f"ld_w1_{i}") for i in range(2)]
        ld_w2 = [sem(f"ld_w2_{i}") for i in range(2)]
        ld_b1 = [sem(f"ld_b1_{i}") for i in range(2)]
        wh_ready = [sem(f"wh_ready_{i}") for i in range(2)]

        block = ctx.enter_context(nc.Block())
        N_X, N_FIRST, N_ATTN, N_LATE = 2, 5, 12, 6

        FIRST = ["k", "q", "ksum", "zb", "zf", ("rep", 0), ("rep", 1), "gh", ("rep", 2), ("rep", 3), ("rep", 4), "g2",
                 ("rep", 5), ("rep", 6)]
        FRONT = (FIRST + [("rep", 7), ("rep", 8), ("rep", 9), ("tr", 0), ("tr", 1)]
                 + [item for m in range(2, 8) for item in (("rep", m + 8), ("tr", m))],
                 FIRST + [("tr", m) for m in range(4)] + [("rep", n) for n in range(7, DH + 4)]
                 + [("tr", m) for m in range(4, 8)] + [("rep", n) for n in range(DH + 4, 2 * DH)])
        def front_bank(b, item):
            return FRONT[b].index(item) % 4

        def front_read(item, b):
            if isinstance(item, tuple):
                kind, n = item
                return ("rep_used", 16 * b + n + 1) if kind == "rep" else ("m_ready", 8 * b + n + 1)
            return {"q": "qcp_ready", "k": "kcp_ready", "zb": "beta_ready", "zf": "f_ready", "ksum": "kinv_ready",
                    "gh": "ghc_ready", "g2": "gate_ready"}[item], b + 1

        def h_bank(b, n):
            return n % 2 if b == 0 else (0, 1, 6, 7)[n % 4]

        def y_bank(u):
            return 2 + u % 2

        TAIL = dict(solutions=21, head_outputs=22, head_squares=25, attn_projection=27, x1_rows=29,
                    x1_transposes=31, cross_queries=32, score_maxima=33, maxima=41, scores=44, head_rows=47,
                    norm_transposes=48, cross_projection=49, x2_rows=51, x2_transposes=53, logits=54,
                    weigh=55, gate_transposes=58, bias_rows=59)
        LAST_BANKS = (3, 4, 5, 0)
        GATES_0 = 1

        POOL_ROW, POOL_COLUMNS = 5, 4

        def update_rows(engine, scratch, k, i0, i1, step, halves=(0, 1), signal="pool_rows"):
            ni, nj = i1 - i0, DH + 1 - i0
            upd = scratch[:, 0:ni * nj * G].rearrange("p (i j g) -> p i j g", i=ni, j=nj)
            if 0 in halves:
                step(engine.tensor_tensor(upd, bc(M[:, k, i0:i1, :], 2, nj), bc(U[:, k, i0 - 1:, :], 1, ni), ALU.mult))
            if 1 in halves:
                step(engine.tensor_tensor(M[:, i0:i1, i0:, :], M[:, i0:i1, i0:, :], upd, ALU.subtract), signal)

        @block.sync
        def _(sp):
            for n, (dst, src) in enumerate((
                    (wqkv_sb[:], wqkv), (xT_sb[:, 0], xT[:, 0]), (wsmall_sb[:], wsmall), (cols_sb[:], cols),
                    (const_sb[:, 0:2 * P], consts[:, 0:2 * P]), (gw2_sb[:], gw2), (rows_sb[:, 0:D], rowsb[0]),
                    (ctxT_sb[:], ctxT), (xT_sb[:, 1], xT[:, 1]), (const_sb[:, 2 * P:], consts[:, 2 * P:]),
                    (x_sb[:], xTok), (wo_sb[:], wo))):
                sp.dma_start(dst, src).then_inc(s["ld_x" if n < N_X else "ld_first" if n < N_FIRST else "ld_attn"], 16)
            for dst, src in ((rows_sb[:, D:2 * D], rowsb[1]), (rows_sb[:, 2 * D:3 * D], rowsb[2]),
                             (rows_sb[:, 3 * D:], rowsb[3]), (xw_sb, xw), (keysrw_sb, keysrw), (b2_sb, b2)):
                sp.dma_start(dst[:], src).then_inc(s["ld_late"], 16)

            def of(t, e, names):
                return t[e] if isinstance(e, int) else t[bass.ds(e, 1)].rearrange(f"o p {names} -> (o p) {names}")

            def first_weights(k, e, done):
                sp.wait_ge(s["ws_ready"], done)
                sp.dma_start(w1_sb[:, k, :], of(w1T, e, "n")).then_inc(ld_w1[k], 16)

            def second_weights(k, e, done, gelus):
                sp.wait_ge(s["gelu_ready"], gelus)
                sp.dma_start(b1_sb[:, k, :], of(b1T, e, "n")).then_inc(ld_b1[k], 16)
                sp.wait_ge(s["y_ready"], done)
                sp.dma_start(w2_sb[:, k, :, :], of(w2T, e, "c n")).then_inc(ld_w2[k], 16)

            def loop_weights(b, i, k):
                second_weights(k, sp.snap(i * 2 + k), sp.snap(i * 2 + (E * b + k - 1)),
                               sp.snap(i * (2 * FC) + FC * (E * b + k - 1)))
                first_weights(k, sp.snap(i * 2 + (k + 2)), sp.snap(i * 2 + (E * b + k + 1)))

            sp.wait_ge(s["rep_used"], 24)
            for k in range(2):
                sp.dma_start(w1_sb[:, k, :], w1T[k]).then_inc(ld_w1[k], 16)
                sp.dma_start(b1_sb[:, k, :], b1T[k]).then_inc(ld_b1[k], 16)
            for k in range(2):
                first_weights(k, 2 + k, 1 + k)
            sp.wait_ge(s["rep_used"], 32)
            for k in range(2):
                sp.dma_start(w2_sb[:, k, :, :], w2T[k]).then_inc(ld_w2[k], 16)
            with sp.Fori(1, E // 2 - 1) as i:
                for k in range(2):
                    loop_weights(0, i, k)
            for k in range(2):
                second_weights(k, E - 2 + k, E - 3 + k, FC * (E - 3 + k))
                first_weights(k, k, E - 1 + k)
            with sp.Fori(0, E // 2 - 1) as i:
                for k in range(2):
                    loop_weights(1, i, k)
            for k in range(2):
                second_weights(k, E - 2 + k, 2 * E - 3 + k, FC * (2 * E - 3 + k))
            for b in range(B):
                sp.wait_ge(s["fin_ready"], TB * (b + 1))
                sp.dma_start(out[:, b], fin[:, b]).then_inc(s["out_done"], 16)
            sp.wait_ge(s["out_done"], 16 * B)

        @block.tensor
        def _(pe):
            mm = nc.tensor.matmul

            def inc(ins, name):
                ins.then_inc(s[name], 1)

            def keep_warm(bank, n):
                for _ in range(n):
                    mm(PS[:, bank, :], ident, xT_sb[:, 0, :], start=True, stop=True)

            def front(b, item):
                n = FRONT[b].index(item)
                bank = n % 4
                before = FRONT[b][bank:n:4]
                if before:
                    name, value = front_read(before[-1], b)
                    pe.wait_ge(s[name], value)
                elif b:
                    name, value = front_read(FRONT[b - 1][bank::4][-1], b - 1)
                    pe.wait_ge(s[name], value)
                xt = xT_sb[:, b, :]
                o = PS[:, bank, :]
                if item == "q":
                    for t in range(TB):
                        last = mm(o[:, t * P:(t + 1) * P], xt[:, t * P:(t + 1) * P], wq, start=True, stop=True)
                    inc(last, "q_ready")
                elif item == "k":
                    inc(mm(o, wqkv_sb[:, 1, :], xt, start=True, stop=True), "k_ready")
                elif item == "zb":
                    inc(mm(o, wfb[:, 1, :], xt, start=True, stop=True), "zb_ready")
                elif item == "zf":
                    inc(mm(o, wfb[:, 0, :], xt, start=True, stop=True), "zf_ready")
                elif item == "ksum":
                    pe.wait_ge(s["ksq_ready"], b + 1)
                    inc(mm(o, headones, sq, start=True, stop=True), "ksum_ready")
                elif item == "gh":
                    inc(mm(o[0:DH, :], gw1, xt, start=True, stop=True), "gh_ready")
                elif item == "g2":
                    pe.wait_ge(s["ghc_ready"], b + 1)
                    inc(mm(o, gw2_sb[:], gateh, start=True, stop=True), "g2_ready")
                elif item[0] == "rep":
                    kv, j = divmod(item[1], DH)
                    if (b, item) == (0, ("rep", DH)):
                        pe.wait_ge(s["wrepv_ready"], 1)
                    inc(mm(o, wrep[:, kv, j, :], xt, start=True, stop=True), "rep_ready")
                else:
                    half, t = divmod(item[1], TB)
                    pe.wait_ge(s["kk_ready"], DH * b + 4 * (half + 1))
                    for jj in range(4):
                        last = nc.tensor.transpose(o[:, jj * P:(jj + 1) * P],
                                                   Akk[:, 4 * half + jj, t * P:(t + 1) * P], ident)
                    inc(last, "tr_ready")

            def solutions(b):
                pe.wait_ge(s["solved"], b + 1)
                for t in range(TB):
                    last = nc.tensor.transpose(PS[:, 4, t * P:(t + 1) * P], xsol[:, t * P:(t + 1) * P], ident)
                inc(last, "qsT_ready")

            def head_outputs(b, js):
                for j in js:
                    pe.wait_ge(s["okv_ready"], DH * b + j + 1)
                    last = mm(PS[:, 5, :], sel[:, j, :], Akv[:, j, :], start=(j == 0), stop=(j == DH - 1))
                if j == DH - 1:
                    inc(last, "oT_ready")

            def head_squares(b):
                pe.wait_ge(s["ogsq_ready"], b + 1)
                inc(mm(PS[:, 6, :], headones, osq[:], start=True, stop=True), "ogms_ready")

            def attn_projection(b):
                pe.wait_ge(s["attn_ready"], b + 1)
                for t in range(TB):
                    last = mm(PS[:, 7, t * P:(t + 1) * P], attn[:, t * P:(t + 1) * P], wo_sb[:],
                              start=True, stop=True)
                inc(last, "attny_ready")

            def x1_transposes(b):
                pe.wait_ge(s["x1_ready"], TB * (b + 1))
                for t in range(TB):
                    last = nc.tensor.transpose(PS[:, 4, t * P:(t + 1) * P], x1[:, t, :], ident)
                inc(last, "x1T_ready")

            def cross_queries(b):
                pe.wait_ge(s["x1T_sb"], b + 1)
                for qd in (1, 2, 3, 0):
                    inc(mm(PS[0:96, 4 + qd, :], w3[:, 0, qd, :, :].rearrange("p r n -> p (r n)"), x1T[:],
                           start=True, stop=True), "xq_ready")

            def score_maxima(b, ns):
                for n in ns:
                    t, qd = divmod(n, NQ)
                    if n < 2:
                        pe.wait_ge(s["ql_ready"], NQ * (b + 1))
                    else:
                        pe.wait_ge(s["mx_ready"], NQ * TB * b + n - 1)
                    for k in range(2):
                        last = mm(PS[:, 4 + 2 * (n % 2) + k, 0:2 * C], QS[0:96, qd, t * P:(t + 1) * P],
                                  KS[0:96, b, qd, 2 * k:2 * k + 2, :].rearrange("p h c -> p (h c)"),
                                  start=True, stop=True)
                    inc(last, "ms_ready")

            def maxima_transposes(b):
                pe.wait_ge(s["nmx_ready"], b + 1)
                for t in range(TB):
                    last = nc.tensor.transpose(PS[:, 4, t * P:(t + 1) * P], nmx[:, t, :], ident)
                inc(last, "nm_ready")

            def scores(b, i):
                qd, st = divmod(i, 5)
                if i < 2:
                    pe.wait_ge(s["qm_ready"], b + 1)
                else:
                    pe.wait_ge(s["p_ready"], 20 * b + i - 1)
                keys = Kr[:, b, qd, :, :].rearrange("p a n -> p (a n)") if st == 0 else KS[:, b, qd, st - 1, 0:P]
                inc(mm(PS[:, 6 + i % 2, :], keys, QS[:, qd, :], start=True, stop=True), "sc_ready")

            def values(b, i):
                qd, st = divmod(i, 5)
                if st == 0 and qd >= 2:
                    pe.wait_ge(s["ox_sb"], NQ * b + qd - 1)
                pe.wait_ge(s["p_ready"], 20 * b + i + 1)
                if st == 0:
                    last = mm(PS[:, 4 + qd % 2, :], Vr[:, b, qd, :, :].rearrange("p a n -> p (a n)"),
                              Pt[:, i % 4, :], start=True, stop=False, skip_group_check=True)
                else:
                    a = st - 1
                    last = mm(PS[32 * a:32 * a + 32, 4 + qd % 2, :], Vm[:, b, 4 * qd + a, :], Pt[:, i % 4, :],
                              start=False, stop=True, tile_position=(0, 32 * a), skip_group_check=True)
                inc(last, "pv_done")

            def cross_step(b, i):
                values(b, i)
                if i < 18:
                    scores(b, i + 2)

            def head_rows(b):
                for t in range(TB):
                    pe.wait_ge(s["ox_sb"], NQ * (b + 1))
                    for qd in range(NQ):
                        last = nc.tensor.transpose(PS[:, 4 + t, qd * P:(qd + 1) * P],
                                                   Osb[:, qd, t * P:(t + 1) * P], ident)
                    inc(last, "xt_ready")

            def norm_transposes(b):
                pe.wait_ge(s["on_ready"], b + 1)
                for t in range(TB):
                    last = nc.tensor.transpose(
                        PS[:, 4, t * P:(t + 1) * P],
                        On[:, t * H:(t + 1) * H, :].rearrange("p h k -> p (h k)"), ident)
                inc(last, "onT_ready")

            def cross_projection(b):
                pe.wait_ge(s["onT_sb"], b + 1)
                for t in range(TB):
                    last = mm(PS[:, 5, t * P:(t + 1) * P], OnT[:, t * P:(t + 1) * P], xwo, start=True, stop=True)
                inc(last, "xy_ready")

            def x2_transposes(b):
                pe.wait_ge(s["x2_ready"], TB * (b + 1))
                for t in range(TB):
                    last = nc.tensor.transpose(PS[:, 6, t * P:(t + 1) * P], x2[:, b, t, :], ident)
                inc(last, "x2T_ready")

            def logits(b):
                pe.wait_ge(s["rc_ready"], 1)
                pe.wait_ge(s["x2L_ready"], b + 1)
                for t in range(TB):
                    o, blk = PS[:, 7, t * E:(t + 1) * E], slice(t * P, (t + 1) * P)
                    mm(o, x2H[:, b, blk], rcH[:], start=True, stop=False)
                    mm(o, x2H[:, b, blk], rcL[:], start=False, stop=False)
                    last = mm(o, x2L[:, b, blk], rcH[:], start=False, stop=True)
                inc(last, "lg_ready")

            def gate_transposes(b):
                pe.wait_ge(s["g_ready"], b + 1)
                for t in range(TB):
                    last = nc.tensor.transpose(PS[0:E, 4, t * P:(t + 1) * P], gates[:, b * TB + t, :], ident)
                inc(last, "gT_ready")

            def bias_rows(b):
                pe.wait_ge(s["gT_sb"], b + 1)
                for t in range(TB):
                    last = mm(PS[:, 5, t * P:(t + 1) * P], gatesT[:, t * P:(t + 1) * P], b2_sb[:], start=True, stop=True)
                inc(last, "acc_in_ready")

            def setup():
                pe.wait_ge(s["ld_late"], 16 * N_LATE)
                pe.wait_ge(s["w3_ready"], 1)
                pe.wait_ge(s["keysq_ready"], 1)
                inc(mm(PS[:, 4, 0:E], onesq[:], keysq[:], start=True, stop=True), "key_ready")
                pe.wait_ge(s["ctxR_ready"], 1)
                for b in range(B):
                    mm(PS[:, 5, b * D:(b + 1) * D], ctxT_sb[:, b, 0:P], xwv, start=True, stop=True)
                    last = mm(PS[:, 5, (B + b) * D:(B + b + 1) * D], ctxR[:, b, :, :].rearrange("p a n -> p (a n)"),
                              xwv, start=True, stop=True)
                inc(last, "vx_ready")
                for qd in range(NQ):
                    if qd >= 2:
                        pe.wait_ge(s["kx_sb"], qd - 1)
                    inc(mm(PS[0:96, 6 + qd % 2, 0:B * C], w3[:, 1, qd, :, :].rearrange("p r n -> p (r n)"),
                           ctxT_sb[:].rearrange("p b c -> p (b c)"), start=True, stop=True), "kx_ready")
                pe.wait_ge(s["kE_sb"], 1)
                pe.wait_ge(s["kx_sb"], NQ)

            def up_chunk(b, u, c, r=0):
                k, n = u % 2, FC * u + c
                if c == 0:
                    pe.wait_ge(s["ws_ready"], r + (E * b + u + 1))
                if b == 0 and n >= 2 or b == 1 and n < 2:
                    pe.wait_ge(s["gelu_ready"], FC * E * b + n - 1)
                elif b == 1 and n >= 4:
                    pe.wait_ge(s["gelu_ready"], r * FC + (FC * E * b + n - 3))
                o, blk = PS[:, h_bank(b, n), :], slice(c * P, (c + 1) * P)
                mm(o, w1H[:, k, blk], x2H[:, b, :], start=True, stop=False)
                mm(o, w1H[:, k, blk], x2L[:, b, :], start=False, stop=False)
                inc(mm(o, w1L[:, k, blk], x2H[:, b, :], start=False, stop=True), "h_ready")

            def down_block(b, u, t, r=0, bank=None):
                if t == 0:
                    pe.wait_ge(ld_w2[u % 2], r * 8 + 16 * ((E * b + u) // 2 + 1))
                    pe.wait_ge(s["gelu_ready"], r * FC + FC * (E * b + u + 1))
                    if E * b + u >= 2:
                        pe.wait_ge(s["acc_done"], r * TB + TB * (E * b + u - 1))
                for c in range(FC):
                    last = mm(PS[:, y_bank(u) if bank is None else bank, t * P:(t + 1) * P],
                              hid[:, u % 2, c, t * P:(t + 1) * P], w2_sb[:, u % 2, c, :],
                              start=(c == 0), stop=(c == FC - 1))
                if bank is not None:
                    inc(last, "last_y_ready")
                elif t == TB - 1:
                    inc(last, "y_ready")

            pe.wait_ge(s["zeros_ready"], 1)
            for _ in range(3):
                mm(PS[:, 7, :], zeros[:, 0:P], zeros, start=True, stop=True)
            pe.wait_ge(s["ld_x"], 16 * N_X)
            for item in FRONT[0][:2]:
                front(0, item)
            pe.wait_ge(s["ld_first"], 16 * (N_FIRST - N_X))
            pe.wait_ge(s["wrep_ready"], 1)
            for item in FRONT[0][2:5]:
                front(0, item)
            pe.wait_ge(s["wrep_ready"], 2)
            for item in FRONT[0][5:11]:
                front(0, item)
            pe.wait_ge(s["ld_attn"], 16 * (N_ATTN - N_FIRST))
            for item in FRONT[0][11:]:
                front(0, item)
            setup()
            for item in ("k", "q", "ksum", "zb", "zf", "gh", "g2"):
                front(1, item)
            pe.wait_ge(s["eliminated"], 1)
            for n in range(3):
                front(1, ("rep", n))
            solutions(0)
            head_outputs(0, range(DH))
            front(1, ("rep", 3))
            head_squares(0)
            front(1, ("rep", 4))
            front(1, ("rep", 5))
            attn_projection(0)
            front(1, ("rep", 6))
            x1_transposes(0)
            cross_queries(0)
            front(1, ("tr", 0))
            front(1, ("tr", 1))
            pe.wait_ge(s["ks_ready"], 1)
            early = {1: ("tr", 2), 3: ("tr", 3), 6: ("rep", 7), 8: ("rep", 8), 11: ("rep", 9)}
            for n in range(NQ * TB):
                score_maxima(0, (n,))
                if n in early:
                    front(1, early[n])
            maxima_transposes(0)
            front(1, ("rep", 10))
            keep_warm(5, 2)
            pe.wait_ge(s["v_ready"], 1)
            early = {1: ("rep", 11), 3: ("tr", 4), 4: ("tr", 5), 8: ("tr", 6), 9: ("tr", 7), 12: ("rep", 12),
                     13: ("rep", 13), 17: ("rep", 14)}
            scores(0, 0)
            scores(0, 1)
            for i in range(20):
                cross_step(0, i)
                if i in early:
                    front(1, early[i])
            head_rows(0)
            norm_transposes(0)
            cross_projection(0)
            front(1, ("rep", 15))
            x2_transposes(0)
            logits(0)
            pe.wait_ge(s["rep_used"], 31)
            pe.wait_ge(s["m_ready"], 16)
            for c in range(FC):
                up_chunk(0, 0, c)
            pe.wait_ge(s["rep_used"], 32)
            tail = {TAIL["solutions"]: [solutions], TAIL["head_outputs"]: [lambda b: head_outputs(b, range(0, 4))],
                    TAIL["head_outputs"] + 1: [lambda b: head_outputs(b, range(4, DH))],
                    TAIL["head_squares"]: [head_squares], TAIL["attn_projection"]: [attn_projection],
                    TAIL["x1_transposes"]: [x1_transposes], TAIL["cross_queries"]: [cross_queries],
                    TAIL["maxima"]: [maxima_transposes], TAIL["head_rows"]: [head_rows],
                    TAIL["norm_transposes"]: [norm_transposes], TAIL["cross_projection"]: [cross_projection],
                    TAIL["x2_transposes"]: [x2_transposes], TAIL["logits"]: [logits],
                    TAIL["gate_transposes"]: [gate_transposes], TAIL["bias_rows"]: [bias_rows]}
            for q in range(E * FC):
                if q == GATES_0:
                    gate_transposes(0)
                if q == GATES_0 + 1:
                    bias_rows(0)
                u, c = divmod(q + FC, FC)
                if q == TAIL["scores"]:
                    scores(1, 0)
                    scores(1, 1)
                    down_block(0, u - 1, 0)
                    for i in range(20):
                        cross_step(1, i)
                        if i in (8, 18):
                            down_block(0, u - 1, 1 + i // 10)
                        if i in (3, 13):
                            up_chunk(0, u, i // 10)
                if not 0 <= q - TAIL["scores"] < 2:
                    up_chunk(*divmod(u, E), c)
                if q == TAIL["scores"]:
                    down_block(0, u - 1, 3)
                if not 0 <= q - TAIL["scores"] < FC:
                    down_block(0, u - 1, c)
                for part in tail.get(q, ()):
                    part(1)
                if 0 <= q - TAIL["score_maxima"] < 8:
                    score_maxima(1, range(2 * (q - TAIL["score_maxima"]), 2 * (q - TAIL["score_maxima"]) + 2))
            with pe.Fori(0, E - 2, 2) as r:
                for u in (0, 1):
                    for c in range(FC):
                        up_chunk(1, u + 1, c, r)
                        down_block(1, u, c, r)
            for c in range(FC):
                up_chunk(1, E - 1, c)
                down_block(1, E - 2, c)
            for t in range(TB):
                down_block(1, E - 1, t, bank=LAST_BANKS[t])

        @block.scalar
        def _(act):
            A = nc.scalar.activation
            count = {}

            def step(ins, name="act_chain"):
                ins.then_inc(s[name], 1)
                count[name] = count.get(name, 0) + 1
                act.wait_ge(s[name], count[name])

            def copy(dst, src, name):
                step(nc.scalar.copy(dst, src), name)

            def norm_tables(norm):
                nc.scalar.preload_act_table_set(LNEXP)
                norm(1)

            def rsqrt(dst, src, name, scale=1.0, eps=L2_EPS):
                step(A(dst, src, ACT.Ln, bias=epst[:, 0:1] if eps == L2_EPS else epst[:, 1:2], scale=scale))
                step(A(dst, dst, ACT.Exp, scale=-0.5), name)

            def query_norms(b):
                act.wait_ge(s["qss_ready"], b + 1)
                rsqrt(qinv[:], qss[:], "qinv_ready")

            def front(b):
                bank = {x: PS[:, front_bank(b, x), :] for x in FRONT[b]}
                act.wait_ge(s["k_ready"], b + 1)
                step(A(sq, bank["k"], ACT.Square), "ksq_ready")
                if b:
                    act.wait_ge(s["kv_ready"], DH * b)
                    nc.scalar.copy(kbeta, bank["k"]).then_inc(s["kcp_ready"], 1)
                act.wait_ge(s["q_ready"], b + 1)
                step(A(qsq, bank["q"], ACT.Square), "qsq_ready")
                act.wait_ge(s["ksum_ready"], b + 1)
                rsqrt(kinv, bank["ksum"], "kinv_ready")
                if b:
                    nc.scalar.copy(qtok, bank["q"]).then_inc(s["qcp_ready"], 1)
                act.wait_ge(s["zb_ready"], b + 1)
                step(A(beta, bank["zb"], ACT.Sigmoid), "beta_ready")
                act.wait_ge(s["zf_ready"], b + 1)
                step(A(fgt[:], bank["zf"], ACT.Sigmoid, bias=delta_col), "f_ready")
                act.wait_ge(s["gh_ready"], b + 1)
                copy(gateh, bank["gh"][0:DH, :], "ghc_ready")
                act.wait_ge(s["g2_ready"], b + 1)
                step(A(gateT[:, b, :], bank["g2"], ACT.Sigmoid), "gate_ready")
                nc.scalar.preload_act_table_set(LNEXP)

            def states(b, ms):
                for m in ms:
                    half, t = divmod(m, TB)
                    act.wait_ge(s["tr_ready"], 2 * TB * b + m + 1)
                    copy(M[:, :, 4 * half:4 * half + 4, t * H:(t + 1) * H].rearrange("p i j h -> p j h i"),
                         PS[:, front_bank(b, ("tr", m)), :].rearrange("p (j h i) -> p j h i", j=4, h=H), "m_ready")

            def head_squares(b):
                act.wait_ge(s["og_ready"], b + 1)
                step(A(osq[:], og[:], ACT.Square), "ogsq_ready")

            def head_norms(b):
                act.wait_ge(s["ogms_ready"], b + 1)
                rsqrt(orr[:], PS[:, 6, :], "ogr_ready", scale=1.0 / DH, eps=NORM_EPS)

            def layer_rstd(n):
                act.wait_ge(s["stats_ready"], n)
                rsqrt(rstd[:], mv[:, :, 1], "rstd_ready", eps=NORM_EPS)

            def x1_columns(b):
                act.wait_ge(s["x1T_ready"], b + 1)
                copy(x1T[:], PS[:, 4, :], "x1T_sb")

            def cross_queries(b):
                for n, qd in enumerate((1, 2, 3, 0)):
                    act.wait_ge(s["xq_ready"], NQ * b + n + 1)
                    step(A(QS[0:96, qd, :], PS[0:96, 4 + qd, :], ACT.Identity, bias=cols_sb[0:96, 3 + qd:4 + qd]),
                         "qh_ready")

            def maxima(b):
                act.wait_ge(s["nm_ready"], b + 1)
                act.wait_ge(s["v_ready"], B)
                copy(mh[96:P, :], PS[96:P, 4, :], "mh_ready")

            def exps(b, i):
                act.wait_ge(s["sc_ready"], 20 * b + i + 1)
                if i >= 4:
                    act.wait_ge(s["pv_done"], 20 * b + i - 3)
                step(A(Pt[:, i % 4, :], PS[:, 6 + i % 2, :], ACT.Exp, scale=SM_SCALE), "p_ready")

            def norm_columns(b):
                act.wait_ge(s["onT_ready"], b + 1)
                copy(OnT[:], PS[:, 4, :], "onT_sb")

            def token_squares(b):
                act.wait_ge(s["x2_ready"], TB * (b + 1))
                for t in range(TB):
                    step(A(osq[:, t * P:(t + 1) * P], x2[:, b, t, :], ACT.Square, accum_out=xsq[:, t:t + 1]),
                         "xsq_ready")

            def x2_columns(b):
                act.wait_ge(s["x2T_ready"], b + 1)
                copy(x2H[:, b, :], PS[:, 6, :], "x2H_ready")

            def top_weights(b):
                act.wait_ge(s["w4_diff"], b + 1)
                step(A(w4[:], w4[:], ACT.Exp), "w4_ready")

            def gate_columns(b):
                act.wait_ge(s["gT_ready"], b + 1)
                copy(gatesT, PS[0:E, 4, :], "gT_sb")

            def gelu_chunk(b, u, c, r=0):
                n = FC * u + c
                act.wait_ge(s["h_ready"], r * FC + (FC * E * b + n + 1))
                if c == 0:
                    act.wait_ge(ld_b1[u % 2], r * 8 + 16 * ((E * b + u) // 2 + 1))
                    if E * b + u >= 2:
                        act.wait_ge(s["y_ready"], r + (E * b + u - 1))
                A(hid[:, u % 2, c, :], PS[:, h_bank(b, n), :], ACT.Gelu, bias=b1_sb[:, u % 2, c:c + 1]).then_inc(
                    s["gelu_ready"], 1)

            nc.scalar.preload_act_table_set(LNEXP)
            act.wait_ge(s["pool_set"], 1)
            act.wait_ge(s["ld_first"], 16 * (N_FIRST - N_X))
            front(0)
            act.wait_ge(s["ld_attn"], 16 * (N_ATTN - N_FIRST))
            step(A(softtmp, lamb_row, ACT.Abs))
            step(A(softtmp, softtmp, ACT.Exp, scale=-1.0))
            step(A(softtmp, softtmp, ACT.Ln, bias=1.0), "lamb_ln")
            query_norms(0)
            act.wait_ge(s["ld_late"], 16 * N_LATE)
            step(A(keysq[:], keysrw_sb[:, 0, :], ACT.Square), "keysq_ready")
            states(0, range(8))
            act.wait_ge(s["key_ready"], 1)
            copy(kE, PS[:, 4, 0:E], "kE_sb")
            act.wait_ge(s["vx_ready"], 1)
            copy(vx.rearrange("p k b n -> p (k b n)"), PS[:, 5, :], "vx_sb")
            for qd in range(NQ):
                act.wait_ge(s["kx_ready"], qd + 1)
                step(A(kx[0:96, qd, :], PS[0:96, 6 + qd % 2, 0:B * C], ACT.Identity,
                       bias=cols_sb[0:96, 3 + NQ + qd:4 + NQ + qd]), "kx_sb")
            front(1)
            act.wait_ge(s["kxS_ready"], 1)
            for b in range(B):
                for qd in range(NQ):
                    for a in range(4):
                        A(KS[:, b, qd, a, :], f(kxS[:, qd, b * C:(b + 1) * C]), ACT.Copy,
                          scale=hmask[:, qd, a:a + 1]).then_inc(s["act_chain"], 1)
                        count["act_chain"] += 1
                act.wait_ge(s["act_chain"], count["act_chain"])
                copy(Kr[:, b, :, :, 0:CR].rearrange("p q a n -> p (q a) n"),
                     f(KS[:, b, :, :, P:C]).rearrange("p q a n -> p (q a) n"), "ks_ready")
            query_norms(1)
            head_squares(0)
            head_norms(0)
            layer_rstd(1)
            x1_columns(0)
            cross_queries(0)
            states(1, range(4))
            maxima(0)
            for i in range(20):
                exps(0, i)
            norm_columns(0)
            layer_rstd(2)
            x2_columns(0)
            token_squares(0)
            top_weights(0)
            for c in range(FC):
                gelu_chunk(0, 0, c)
            tail = {TAIL["head_squares"] - 2: [head_squares], TAIL["head_squares"]: [lambda b: norm_tables(head_norms)],
                    TAIL["x1_rows"]: [lambda b: norm_tables(lambda b: layer_rstd(3))], TAIL["x1_transposes"]: [x1_columns],
                    TAIL["cross_queries"]: [cross_queries], TAIL["maxima"]: [maxima],
                    TAIL["norm_transposes"]: [norm_columns],
                    TAIL["x2_rows"]: [lambda b: norm_tables(lambda b: layer_rstd(4))],
                    TAIL["x2_transposes"]: [x2_columns, token_squares],
                    TAIL["weigh"]: [top_weights], TAIL["gate_transposes"]: [gate_columns]}
            for q in range(E * FC):
                u, c = divmod(q + FC, FC)
                if q == GATES_0:
                    gate_columns(0)
                if q == TAIL["scores"]:
                    for i in range(20):
                        exps(1, i)
                gelu_chunk(*divmod(u, E), c)
                for part in tail.get(q, ()):
                    part(1)
            norm_tables(lambda b: layer_rstd(5))
            nc.scalar.preload_act_table_set(GELU_SET)
            with act.Fori(0, E - 2, 2) as r:
                for u in (1, 2):
                    for c in range(FC):
                        gelu_chunk(1, u, c, r)
            for c in range(FC):
                gelu_chunk(1, E - 1, c)
            norm_tables(lambda b: layer_rstd(6))

        @block.gpsimd
        def _(pool):
            Gp = nc.gpsimd
            count = {}

            def step(ins, name="pool_chain"):
                ins.then_inc(s[name], 1)
                count[name] = count.get(name, 0) + 1
                pool.wait_ge(s[name], count[name])

            Gp.memset(epst[:, 0:1], L2_EPS)
            step(Gp.memset(epst[:, 1:2], NORM_EPS), "pool_set")
            pool.wait_ge(s["ld_first"], 16 * (N_FIRST - N_X))
            step(Gp.tensor_copy(wrep[:, 1, :, :].rearrange("p j (h i) -> p j h i", h=H),
                                bc(wqkv_sb[:, 2, :].rearrange("p (h j) -> p j h", h=H), 3, DH)), "wrepv_ready")
            Gp.memset(onesq[:], 1.0)
            Gp.memset(f(Kr[:]), 0.0)
            Gp.memset(Vr[:], 0.0)
            Gp.memset(nmx[:], 0.0)
            Gp.memset(Vm[:], 0.0)
            step(Gp.memset(ctxR, 0.0))
            pool.wait_ge(s["ld_attn"], 16 * (N_ATTN - N_FIRST))
            step(Gp.tensor_copy(ctxR[:, :, :, 0:CR], bc(ctxT_sb[:, :, P:C], 2, 4)), "ctxR_ready")
            pool.wait_ge(s["lamb_ln"], 1)
            step(Gp.tensor_scalar(lamb[:], lamb_row, 0.0, LAMBDA_LOWER, ALU.max, ALU.add))
            step(Gp.tensor_tensor(lamb[:], lamb[:], softtmp, ALU.add), "lamb_ready")
            pool.wait_ge(s["ld_late"], 16 * N_LATE)
            for k in range(2):
                last = Gp.tensor_copy(w3[:, k], bc(xw_sb[:, k, :].rearrange("p (q n) -> p q n", q=NQ), 2, 3))
                if k == 0:
                    step(last)
            step(last, "w3_ready")
            step(Gp.tensor_scalar(rcomb[:], keysrw_sb[:, 0, :], 2.0, None, ALU.mult))
            step(Gp.tensor_tensor(rcomb[:], rcomb[:], keysrw_sb[:, 1, :], ALU.add))
            step(Gp.tensor_copy(rcH[:], rcomb[:]))
            step(Gp.tensor_tensor(rcL[:], rcomb[:], f(rcH[:]), ALU.subtract), "rc_ready")
            pool.wait_ge(s["kE_sb"], 1)
            step(Gp.tensor_tensor(cE[:], rb_row, kE, ALU.subtract), "cE_ready")
            for k in range(POOL_COLUMNS):
                pool.wait_ge(s["factor_row"], k + 1)
                update_rows(Gp, acc[:].rearrange("p b t d -> p (b t d)"), k, POOL_ROW, DH, step)
            pool.wait_ge(s["kx_sb"], NQ)
            step(Gp.tensor_copy(kxS[0:96], kx[0:96]))
            step(Gp.memset(f(kxS[96:P]), 1.0))
            step(Gp.tensor_tensor(kxS[32:64], kx[32:64], f(kxS[32:64]), ALU.subtract), "kxS_ready")
            pool.wait_ge(s["vx_sb"], 1)
            for b in range(B):
                step(Gp.tensor_tensor(Vm[:, b, :, 0:DH], vx[:, 0, b, :].rearrange("p (h k) -> p h k", h=H),
                                      bv_row.rearrange("p (h k) -> p h k", h=H), ALU.add))
                step(Gp.memset(Vm[:, b, :, DH:DH + 1], 1.0))
                for a in range(4):
                    rows = slice(32 * a, 32 * a + CR)
                    step(Gp.tensor_tensor(
                        Vr[rows, b, :, a, 0:DH],
                        vx[rows, 1, b, :].rearrange("p (q a k) -> p q a k", q=NQ, a=4)[:, :, a, :],
                        bv_row[rows, :].rearrange("p (q a k) -> p q a k", q=NQ, a=4)[:, :, a, :], ALU.add))
                    last = Gp.memset(Vr[rows, b, :, a, DH:DH + 1], 1.0)
                    if a < 3:
                        step(last)
                step(last, "v_ready")
            def split(k, n):
                def chunks(w):
                    return w[:, k, :].rearrange("p (c n) -> p c n", c=FC)

                pool.wait_ge(ld_w1[k], n * 16 + 16)
                Gp.tensor_tensor(chunks(w1H), chunks(w1_sb), bc(onesq[:], 1, FC), ALU.mult).then_inc(wh_ready[k], 1)
                pool.wait_ge(wh_ready[k], n + 1)
                Gp.tensor_tensor(w1L[:, k, :], w1_sb[:, k, :], f(w1H[:, k, :]), ALU.subtract).then_inc(
                    s["ws_ready"], 1)

            for k in range(2):
                split(k, 0)
            with pool.Fori(1, B * E // 2) as n:
                for k in range(2):
                    pool.wait_ge(s["h_ready"], n * (2 * FC) + (FC * (k - 1)))
                    split(k, n)

        @block.vector
        def _(dve):
            V = nc.vector
            count = {}

            def step(ins, name="dve_chain"):
                ins.then_inc(s[name], 1)
                count[name] = count.get(name, 0) + 1
                dve.wait_ge(s[name], count[name])

            def emit(ins, name="dve_chain"):
                ins.then_inc(s[name], 1)
                count[name] = count.get(name, 0) + 1

            def tt(o, a, c, op, name="dve_chain"):
                step(V.tensor_tensor(o, a, c, op), name)

            def flat(ap):
                return ap.rearrange("p t d -> p (t d)")

            def layer_stats(src=res, stats_done=False):
                for t in range(0 if stats_done else TB):
                    (step if t == TB - 1 else emit)(V.bn_stats(stats[:, t, :], src[:, t, :]))
                for t in range(TB):
                    last = V.bn_aggr(mv[:, t, :], stats[:, t, :])
                step(last, "stats_ready")

            def normalise(dst, signal, src=res):
                dve.wait_ge(s["rstd_ready"], count["stats_ready"])
                for t in range(TB):
                    (step if t == TB - 1 else emit)(
                        V.tensor_scalar(dst[:, t, :], src[:, t, :], mv[:, t, 0:1], rstd[:, t:t + 1],
                                        ALU.subtract, ALU.mult), signal)

            def key_vectors(b):
                dve.wait_ge(s["qsq_ready"], b + 1)
                step(V.tensor_reduce(qss[:], qsq.rearrange("p (g i) -> p g i", i=DH), AX.X, ALU.add), "qss_ready")
                dve.wait_ge(s["kcp_ready"], b + 1)
                dve.wait_ge(s["kinv_ready"], b + 1)
                tt(kbeta, kbeta, kinv, ALU.mult)
                dve.wait_ge(s["beta_ready"], b + 1)
                tt(kbeta, kbeta, beta, ALU.mult)
                tt(kc[:], kbeta, kinv, ALU.mult, "kvec_ready")
                dve.wait_ge(s["f_ready"], b + 1)

            def scanned(b, n):
                return ("kk_ready", DH * b + n + 1) if n < DH else ("kv_ready", DH * (b - 1) + n + 1)

            def product(b, n, dst):
                dve.wait_ge(s["rep_ready"], 2 * DH * b + n + 1)
                emit(V.tensor_tensor(dst, (kc if n < DH else kbeta)[:], PS[:, front_bank(b, ("rep", n)), :], ALU.mult),
                     "rep_used")

            def recurrence(b, n, added):
                dve.wait_ge(s["rep_used"], 2 * DH * b + n + 1)
                name, _ = scanned(b, n)
                emit(V.tensor_tensor_scan((Akk if n < DH else Akv)[:, n % DH, :], fgt[:], added, 0.0,
                                          ALU.mult, ALU.add), name)

            def scan(b, n):
                product(b, n, prod)
                recurrence(b, n, prod)
                name, value = scanned(b, n)
                dve.wait_ge(s[name], value)

            def scans(b):
                places = (prod, flat(x2[:, 0]), flat(x2[:, 1]))
                product(b, 0, places[0])
                for n in range(2 * DH):
                    if n < 2 * DH - 1:
                        if n >= 2:
                            name, value = scanned(b, n - 2)
                            dve.wait_ge(s[name], value)
                        product(b, n + 1, places[(n + 1) % 3])
                    recurrence(b, n, places[n % 3])
                    if n == DH:
                        right_sides(b)
                dve.wait_ge(s["kv_ready"], DH * (b + 1))

            def state(b, m):
                half, t = divmod(m, TB)
                dve.wait_ge(s["tr_ready"], 2 * TB * b + m + 1)
                V.tensor_copy(M[:, :, 4 * half:4 * half + 4, t * H:(t + 1) * H].rearrange("p i j h -> p j h i"),
                              PS[:, front_bank(b, ("tr", m)), :].rearrange("p (j h i) -> p j h i", j=4, h=H)).then_inc(
                                  s["m_ready"], 1)
                dve.wait_ge(s["m_ready"], 2 * TB * b + m + 1)

            def right_sides(b):
                dve.wait_ge(s["qinv_ready"], b + 1)
                dve.wait_ge(s["qcp_ready"], b + 1)
                tt(M[:, :, DH, :].rearrange("p i g -> p g i"), qtok.rearrange("p (g i) -> p g i", i=DH),
                   bc(qinv[:], 2, DH), ALU.mult, "qn_ready")

            def diagonal(b):
                dve.wait_ge(s["m_ready"], 8 * (b + 1))
                dve.wait_ge(s["lamb_ready"], 1)
                Md = M[:].rearrange("p i j g -> p (i j) g")[:, 0:DH * (DH + 1):DH + 2, :].rearrange(
                    "p i (t h) -> p i t h", t=TB)
                tt(Md, Md, bc(lamb[:].rearrange("p (h i) -> p i h", h=H), 2, TB), ALU.add)

            def eliminate(b, k, parts=range(5)):
                n = DH - 1 - k
                if (b, k) == (0, POOL_COLUMNS):
                    dve.wait_ge(s["pool_rows"], POOL_COLUMNS)
                if 0 in parts:
                    step(V.reciprocal(rpiv[:], M[:, k, k, :]), "eliminated" if k == DH - 1 else "dve_chain")
                    tt(U[:, k, k:, :], M[:, k, k + 1:, :], bc(rpiv[:], 1, n + 1), ALU.mult,
                       "factor_row" if b == 0 and k < POOL_COLUMNS else "dve_chain")
                end = POOL_ROW if b == 0 and k < POOL_COLUMNS else DH
                cut = k + 1 + ((end - k - 1) // 2 if end - k - 1 >= 4 else end - k - 1)
                for part, i0, i1 in ((1, k + 1, cut), (3, cut, end)):
                    if i1 > i0:
                        update_rows(V, tmp[:], k, i0, i1, step, [p - part for p in parts], "dve_chain")

            def substitute(b):
                y = U[:, :, DH - 1, :]
                for j in range(DH - 1, 0, -1):
                    upd = tmp[:, 0:j * G].rearrange("p (i g) -> p i g", i=j)
                    tt(upd, U[:, 0:j, j - 1, :], bc(y[:, j, :], 1, j), ALU.mult)
                    tt(y[:, 0:j, :], y[:, 0:j, :], upd, ALU.subtract)
                step(V.tensor_copy(xsol[:].rearrange("p (g i) -> p i g", i=DH), y), "solved")

            def outputs(b):
                dve.wait_ge(s["qsT_ready"], b + 1)
                for j in range(DH):
                    emit(V.tensor_tensor(Akv[:, j, :], Akv[:, j, :], PS[:, 4, :], ALU.mult), "okv_ready")

            def gated(b):
                dve.wait_ge(s["oT_ready"], b + 1)
                dve.wait_ge(s["gate_ready"], b + 1)
                tt(og[:], PS[:, 5, :], gateT[:, b, :], ALU.mult, "og_ready")

            def head_normed(b):
                dve.wait_ge(s["ogr_ready"], b + 1)
                step(V.scalar_tensor_tensor(attn[:], og[:], normw_col, orr[:], ALU.mult, ALU.mult), "attn_ready")

            def attn_residual(b):
                dve.wait_ge(s["attny_ready"], b + 1)
                tt(flat(res[:]), flat(x_sb[:, b]), PS[:, 7, :], ALU.add)
                layer_stats()

            def x1_rows(b):
                normalise(x1, "x1_ready")
                tt(x1b, x1, bc(bo_row, 1, TB), ALU.add)

            def cross_queries(b):
                for n, qd in enumerate((1, 2, 3, 0)):
                    dve.wait_ge(s["qh_ready"], NQ * b + n + 1)
                    step(V.scalar_tensor_tensor(QS[64:96, qd, :], PS[64:96, 4 + qd, :], cols_sb[64:96, 3 + qd:4 + qd],
                                                f(QS[64:96, qd, :]), ALU.add, ALU.subtract), "ql_ready")

            def score_maxima(b, ns):
                for n in ns:
                    t, qd = divmod(n, NQ)
                    dve.wait_ge(s["ms_ready"], NQ * TB * b + n + 1)
                    k = 4 + 2 * (n % 2)
                    heads = nmx[:, t, 96 + 8 * qd:100 + 8 * qd].rearrange("p (k h) -> p k h", k=2)
                    tile = PS[:, k:k + 2, 0:2 * C].rearrange("p k (h c) -> p k h c", h=2)
                    (step if n == NQ * TB - 1 else emit)(
                        V.tensor_reduce(heads, tile, AX.X, ALU.max, negate=True), "mx_ready")
                if n < NQ * TB - 1:
                    return
                m = nmx[:, :, 96:].rearrange("p t (q n) -> p t q n", n=8)
                step(V.tensor_copy(m[:, :, :, 4:8], m[:, :, :, 0:4]), "nmx_ready")

            def maxima(b):
                dve.wait_ge(s["mh_ready"], b + 1)
                step(V.scalar_tensor_tensor(mh[96:P, :], f(mh[96:P, :]), lowneg_col[96:P], PS[96:P, 4, :],
                                            ALU.mult, ALU.add))
                step(V.tensor_copy(QS[96:P, :, :], bc(f(mh[96:P, :]), 1, NQ)), "qm_ready")

            def head_sums(b, qd):
                dve.wait_ge(s["pv_done"], 20 * b + 5 * (qd + 1))
                step(V.tensor_copy(Osb[:, qd, :], PS[:, 4 + qd % 2, :]), "ox_sb")

            def head_rows(b):
                dve.wait_ge(s["xt_ready"], TB * (b + 1))
                T = PS[:, 4:8, :].rearrange("p t (h w) -> p (t h) w", w=32)
                step(V.reciprocal(rden[:], T[:, :, DH]))
                tt(On, T[:, :, 0:DH], bc(rden[:], 2, DH), ALU.mult, "on_ready")

            def cross_residual(b):
                dve.wait_ge(s["xy_ready"], b + 1)
                tt(flat(res[:]), flat(x1b), PS[:, 5, :], ALU.add)
                layer_stats()

            def x2_rows(b):
                normalise(x2[:, b], "x2_ready")

            def x2_low(b):
                dve.wait_ge(s["x2H_ready"], b + 1)
                tt(x2L[:, b, :], PS[:, 6, :], f(x2H[:, b, :]), ALU.subtract, "x2L_ready")

            def choose(b):
                dve.wait_ge(s["lg_ready"], b + 1)
                dve.wait_ge(s["cE_ready"], 1)
                tt(logit[:], PS[:, 7, 0:TB * E].rearrange("p (t e) -> p t e", t=TB), bc(cE[:], 1, TB), ALU.add)
                dve.wait_ge(s["xsq_ready"], TB * (b + 1))
                tt(logit[:], logit[:], bc(xsq[:], 2, E), ALU.subtract)
                for t in range(TB):
                    step(V.max(top8[:, t, :], logit[:, t, :]))
                tt(w4[:], top8[:, :, 0:TOPK], bc(top8[:, :, 0], 2, TOPK), ALU.subtract, "w4_diff")
                for t in range(TB):
                    step(V.max_index(idx8[:, t, :], top8[:, t, :], logit[:, t, :]))
                step(V.tensor_copy(idx4[:], idx8[:, :, 0:TOPK]))
                tt(oneh[:], bc(iota, 1, TB * TOPK), bc(idx4[:].rearrange("p t r -> p (t r)"), 2, E), ALU.is_equal)

            def weigh(b):
                dve.wait_ge(s["w4_ready"], b + 1)
                step(V.tensor_reduce(wsum[:], w4[:], AX.X, ALU.add))
                step(V.reciprocal(wsum[:], wsum[:]))
                tt(w4[:], w4[:], bc(wsum[:], 2, TOPK), ALU.mult)
                tt(oneh[:], oneh[:], bc(w4[:].rearrange("p t r -> p (t r)"), 2, E), ALU.mult)
                step(V.tensor_reduce(gates[:, b * TB:(b + 1) * TB, :],
                                     oneh[:].rearrange("p (t r) e -> p t e r", t=TB), AX.X, ALU.add), "g_ready")

            def start_sums(b):
                dve.wait_ge(s["acc_in_ready"], b + 1)
                tt(flat(acc[:, b]), flat(x2[:, b]), PS[:, 5, :], ALU.add, "acc_init")

            def accumulate(b, u, gate, r=0):
                dve.wait_ge(s["y_ready"], r + (E * b + u + 1))
                for t in range(TB):
                    V.scalar_tensor_tensor(acc[:, b, t, :], PS[:, y_bank(u), t * P:(t + 1) * P],
                                           gate[:, t:t + 1], acc[:, b, t, :], ALU.mult, ALU.add).then_inc(
                                               s["acc_done"], 1)

            step(V.memset(zeros, 0.0), "zeros_ready")
            dve.wait_ge(s["ld_first"], 16 * (N_FIRST - N_X))
            step(V.tensor_copy(wfb[:].rearrange("p k (h i) -> p (k h) i", h=H), bc(wsmall_sb[:, 0:2 * H], 2, DH)),
                 "wrep_ready")
            step(V.tensor_copy(wrep[:, 0, :, :].rearrange("p j (h i) -> p j h i", h=H),
                               bc(wqkv_sb[:, 1, :].rearrange("p (h j) -> p j h", h=H), 3, DH)), "wrep_ready")
            dve.wait_ge(s["ksq_ready"], 1)
            step(V.tensor_copy(kbeta, PS[:, front_bank(0, "k"), :]), "kcp_ready")
            dve.wait_ge(s["qsq_ready"], 1)
            step(V.tensor_copy(qtok, PS[:, front_bank(0, "q"), :]), "qcp_ready")
            key_vectors(0)
            scans(0)
            diagonal(0)
            for k in range(DH):
                eliminate(0, k)
            substitute(0)
            outputs(0)
            key_vectors(1)
            scan(1, 0)
            gated(0)
            scan(1, 1)
            scan(1, 2)
            head_normed(0)
            scan(1, 3)
            attn_residual(0)
            x1_rows(0)
            for n in range(4, 7):
                scan(1, n)
            cross_queries(0)
            score_maxima(0, range(NQ * TB))
            scan(1, 7)
            maxima(0)
            right_sides(1)
            scan(1, 8)
            scan(1, 9)
            head_sums(0, 0)
            scan(1, 10)
            scan(1, 11)
            state(1, 4)
            state(1, 5)
            head_sums(0, 1)
            state(1, 6)
            state(1, 7)
            head_sums(0, 2)
            diagonal(1)
            eliminate(1, 0, (0, 1))
            head_sums(0, 3)
            scan(1, 12)
            head_rows(0)
            scan(1, 13)
            eliminate(1, 0, (2,))
            cross_residual(0)
            x2_rows(0)
            scan(1, 14)
            x2_low(0)
            scan(1, 15)
            eliminate(1, 0, (3,))
            choose(0)
            eliminate(1, 0, (4,))
            weigh(0)
            tail = {0: [lambda b: eliminate(b, 1), lambda b: start_sums(0)], 4: [lambda b: eliminate(b, 2)],
                    8: [lambda b: eliminate(b, 3), lambda b: eliminate(b, 4)],
                    12: [lambda b: eliminate(b, 5), lambda b: eliminate(b, 6), lambda b: eliminate(b, 7)]}
            tail |= {16: [substitute], TAIL["solutions"]: [outputs], TAIL["head_outputs"] + 1: [gated],
                    TAIL["head_squares"]: [head_normed], TAIL["attn_projection"]: [attn_residual],
                    TAIL["x1_rows"]: [x1_rows], TAIL["cross_queries"]: [cross_queries], TAIL["maxima"]: [maxima],
                    TAIL["head_rows"]: [head_rows], TAIL["cross_projection"]: [cross_residual],
                    TAIL["x2_rows"]: [x2_rows], TAIL["x2_transposes"]: [x2_low], TAIL["logits"]: [choose],
                    TAIL["weigh"]: [weigh], TAIL["bias_rows"]: [start_sums]}
            for q in range(E * FC):
                if q % FC == FC - 1:
                    if q >= FC:
                        dve.wait_ge(s["acc_done"], TB * (q // FC))
                    accumulate(0, q // FC, gates[:, 0:TB, q // FC])
                for part in tail.get(q, ()):
                    part(1)
                if 0 <= q - TAIL["score_maxima"] < 8:
                    score_maxima(1, range(2 * (q - TAIL["score_maxima"]), 2 * (q - TAIL["score_maxima"]) + 2))
                if q == TAIL["scores"]:
                    for qd in range(NQ):
                        head_sums(1, qd)

            def loop_unit(u, i):
                r = i * 2
                src = gates[:, TB:, :].rearrange("p t (n u) -> p t n u", u=2)[:, :, bass.ds(i, 1), u]
                V.tensor_copy(gslot[:, u, :], src.rearrange("p t o -> p (t o)")).then_inc(s["gslot_ready"], 1)
                dve.wait_ge(s["gslot_ready"], r + (u + 1))
                accumulate(1, u, gslot[:, u, :], r)
                dve.wait_ge(s["acc_done"], r * TB + TB * (E + u + 1))

            def output(b, stats_done=False):
                if not stats_done:
                    dve.wait_ge(s["acc_done"], TB * E * (b + 1))
                layer_stats(acc[:, b], stats_done)
                normalise(fin[:, b], "fin_ready", acc[:, b])

            output(0)
            with dve.Fori(0, E // 2 - 1) as i:
                loop_unit(0, i)
                loop_unit(1, i)
            accumulate(1, E - 2, gates[:, TB:, E - 2])
            dve.wait_ge(s["acc_done"], TB * (2 * E - 1))
            for t in range(TB):
                dve.wait_ge(s["last_y_ready"], t + 1)
                V.scalar_tensor_tensor(acc[:, 1, t, :], PS[:, LAST_BANKS[t], t * P:(t + 1) * P],
                                       gates[:, TB + t, E - 1:E], acc[:, 1, t, :], ALU.mult, ALU.add).then_inc(
                                           s["acc_done"], 1)
                dve.wait_ge(s["acc_done"], TB * (2 * E - 1) + t + 1)
                (step if t == TB - 1 else emit)(V.bn_stats(stats[:, t, :], acc[:, 1, t, :]))
            output(1, stats_done=True)


_OUTS = [((B, S, D), "float32")]


def kernel(**inputs):
    import numpy as np
    import concourse.bacc as bacc
    from concourse.bass_utils import run_bass_kernel_spmd

    a = {k: np.asarray(v) for k, v in inputs.items()}

    def w(name):
        return a["L0_" + name]

    def token_blocks(v):
        return v.reshape(B, TB, P, D).transpose(2, 0, 1, 3)

    r = np.arange(P)
    cols = np.zeros((P, 3 + 2 * NQ), np.float32)
    cols[:, 0] = np.repeat(w("attn_delta"), DH)
    cols[:, 1] = w("attn_norm_weight")
    cols[96:, 2] = -(r[96:] % 8 // 4)
    cols[0:96, 3:3 + NQ] = np.tile(w("xattn_bq").reshape(NQ, 32).T, (3, 1))
    cols[0:96, 3 + NQ:] = np.tile(w("xattn_bk").reshape(NQ, 32).T, (3, 1))
    consts = np.zeros((P, 2 * P + DH * P + NQ * 4 + E), np.float32)
    consts[:, 0:P] = np.eye(P)
    consts[:, P:2 * P] = r[:, None] // DH == r[None, :] // DH
    for j in range(DH):
        consts[:, 2 * P + j * P:2 * P + (j + 1) * P] = (r[:, None] // DH == r[None, :] // DH) & (r[None, :] % DH == j)
    hm = consts[:, 2 * P + DH * P:2 * P + DH * P + NQ * 4].reshape(P, NQ, 4)
    hm[0:96] = (r[0:96] % 32 // DH)[:, None, None] == np.arange(4)
    hm[96:] = ((r[96:] - 96) // 8)[:, None, None] == np.arange(NQ)[:, None]
    hm[96:] *= (r[96:] % 4)[:, None, None] == np.arange(4)
    consts[:, 2 * P + DH * P + NQ * 4:] = np.arange(E)
    consts[:, 2 * P + DH * P:2 * P + DH * P + NQ * 4] = hm.reshape(P, NQ * 4)
    arrays = {
        "xTok": token_blocks(a["x"]),
        "xT": a["x"].transpose(2, 0, 1),
        "ctxT": a["ctx_1024"].transpose(2, 0, 1),
        "wqkv": np.stack([w("attn_Wq"), w("attn_Wk"), w("attn_Wv")], 1),
        "wsmall": np.concatenate([w("attn_Wf"), w("attn_Wbet"), w("attn_gate_w1")], 1),
        "gw2": w("attn_gate_w2"),
        "wo": w("attn_Wo"),
        "cols": cols,
        "lamb": w("attn_lamb_params"), "bv": w("xattn_bv"), "bo": w("xattn_bo"), "rb": w("ffn_rb"),
        "xw": np.stack([w("xattn_Wq"), w("xattn_Wk"), w("xattn_Wv"), w("xattn_Wo")], 1),
        "keysrw": np.stack([w("ffn_keys").T, w("ffn_rw").T], 1),
        "b2": w("ffn_b2"),
        "w1T": w("ffn_w1").transpose(0, 2, 1),
        "w2T": w("ffn_w2").transpose(0, 2, 1).reshape(E, FC, P, D).transpose(0, 2, 1, 3),
        "b1T": w("ffn_b1").reshape(E, FC, P).transpose(0, 2, 1),
        "consts": consts,
    }
    arrays = {k: np.ascontiguousarray(v) for k, v in arrays.items()}
    nc = bacc.Bacc("TRN2", target_bir_lowering=False, num_devices=1)
    t = {k: nc.dram_tensor(f"in_{k}", v.shape, F32, kind="ExternalInput").ap() for k, v in arrays.items()}
    out = nc.dram_tensor("out", (B, S, D), F32, kind="ExternalOutput").ap()
    rows = [t.pop(k).rearrange("(o n) -> o n", o=1).broadcast_to((P, n))
            for k, n in (("lamb", D), ("bv", D), ("bo", D), ("rb", E))]
    decoder_layer(nc, rowsb=rows, out=out.rearrange("b (t p) d -> p b t d", p=P), **t)
    r = run_bass_kernel_spmd(nc, [{f"in_{k}": v for k, v in arrays.items()}], core_ids=[0])
    return r.results[0]["out"]
```
